# Optimizing a Trainium2 kernel written in Bass

```python
import numpy as np
import jax
import jax.numpy as jnp

def _softmax(x, axis=-1):
    return jax.nn.softmax(x, axis=axis)

def _gelu(x):
    return jax.nn.gelu(x, approximate=True)

def _silu(x):
    return jax.nn.silu(x)

def _sigmoid(x):
    return jax.nn.sigmoid(x)

def _layernorm(x, axis=-1, eps=1e-05):
    m = jnp.mean(x, axis=axis, keepdims=True)
    v = jnp.var(x, axis=axis, keepdims=True)
    return (x - m) / jnp.sqrt(v + eps)

def _scatter_add(tgt, idx, src, axis=0):
    return tgt.at[idx].add(src)

def _segment_sum(src, seg, n):
    return jax.ops.segment_sum(src, seg, n)
kernel_name = 'mk_adaln_d2_jaxref_r8_7bc368'

def setup_inputs(seed: int=0):
    np.random.seed(seed)
    _w = jnp.asarray

    def _L0_attn_setup():
        import jax, jax.numpy as jnp
        import numpy as np
        HID = 128
        NH = 16
        NKV = 4
        HD = 64
        C = 64
        RATIO = 0.125
        KS = 7

        def _block_causal_attention(x, qw, kw, vw, ow, k):
            B, nc, _, D = x.shape
            T = nc * k
            xf = x.reshape(B, T, D)
            q = (xf @ qw.T).reshape(B, T, NH, HD).transpose(0, 2, 1, 3)
            kk = (xf @ kw.T).reshape(B, T, NKV, HD).transpose(0, 2, 1, 3)
            v = (xf @ vw.T).reshape(B, T, NKV, HD).transpose(0, 2, 1, 3)
            rep = NH // NKV
            kk = jnp.repeat(kk, rep, axis=1)
            v = jnp.repeat(v, rep, axis=1)
            chunk_ids = jnp.arange(T) // k
            mask = chunk_ids[:, None] >= chunk_ids[None, :]
            scores = jnp.einsum('bhqd,bhkd->bhqk', q, kk) / np.float32(np.sqrt(HD))
            scores = jnp.where(mask[None, None], scores, jnp.finfo(scores.dtype).min)
            p = jax.nn.softmax(scores, axis=-1)
            o = jnp.einsum('bhqk,bhkd->bhqd', p, v)
            o = o.transpose(0, 2, 1, 3).reshape(B, T, NH * HD)
            return (o @ ow.T).reshape(B, nc, k, D)

        def _causal_conv(x, dw, pw):
            B, nc, L, D = x.shape
            xc = x.reshape(B * nc, L, D).transpose(0, 2, 1)
            xp = jnp.pad(xc, ((0, 0), (0, 0), (KS - 1, 0)))
            y = jax.lax.conv_general_dilated(xp, dw, window_strides=(1,), padding='VALID', dimension_numbers=('NCH', 'OIH', 'NCH'), feature_group_count=D)
            y = jax.nn.gelu(y, approximate=False)
            y = jnp.einsum('ncl,oc->nol', y, pw)
            return y.transpose(0, 2, 1).reshape(B, nc, L, D)

        def _forward(hidden_states, q_w, k_w, v_w, o_w, dw_r, pw_r, dw_i, pw_i, gate_w, alpha_raw):
            B, N, D = hidden_states.shape
            pad_len = -N % C
            x = jnp.pad(hidden_states, ((0, 0), (0, pad_len), (0, 0))) if pad_len else hidden_states
            nc = x.shape[1] // C
            chunks = x.reshape(B, nc, C, D)
            Xh = jnp.fft.rfft(chunks.astype(jnp.float32), axis=2)
            M = Xh.shape[2]
            k = max(1, int(M * RATIO))
            X_low, X_high = (Xh[:, :, :k, :], Xh[:, :, k:, :])
            A_r = _block_causal_attention(X_low.real, q_w, k_w, v_w, o_w, k)
            A_i = _block_causal_attention(X_low.imag, q_w, k_w, v_w, o_w, k)
            A_low = jax.lax.complex(A_r, A_i)
            H_r = _causal_conv(X_high.real, dw_r, pw_r)
            H_i = _causal_conv(X_high.imag, dw_i, pw_i)
            g = jax.nn.sigmoid(chunks.mean(axis=2) @ gate_w.T)[:, :, None, :]
            A_high = jax.lax.complex(H_r * g, H_i * g) + X_high
            alpha = jax.nn.sigmoid(alpha_raw)
            A_low_fused = alpha * A_low + (1.0 - alpha) * X_low
            Y_hat = jnp.concatenate([A_low_fused, A_high], axis=2)
            Y = jnp.fft.irfft(Y_hat, n=C, axis=2)
            return Y.reshape(B, -1, D)[:, :N, :].astype(hidden_states.dtype)
        key = jax.random.key(seed)
        ks = jax.random.split(key, 11)
        B, N = (4, 512)
        s = 0.02
        return {'hidden_states': jax.random.normal(ks[0], (B, N, HID), jnp.float32), 'q_w': jax.random.normal(ks[1], (NH * HD, HID), jnp.float32) * s, 'k_w': jax.random.normal(ks[2], (NKV * HD, HID), jnp.float32) * s, 'v_w': jax.random.normal(ks[3], (NKV * HD, HID), jnp.float32) * s, 'o_w': jax.random.normal(ks[4], (HID, NH * HD), jnp.float32) * s, 'dw_r': jax.random.normal(ks[5], (HID, 1, KS), jnp.float32) * 0.3, 'pw_r': jax.random.normal(ks[6], (HID, HID), jnp.float32) * s, 'dw_i': jax.random.normal(ks[7], (HID, 1, KS), jnp.float32) * 0.3, 'pw_i': jax.random.normal(ks[8], (HID, HID), jnp.float32) * s, 'gate_w': jax.random.normal(ks[9], (HID, HID), jnp.float32) * s, 'alpha_raw': jnp.zeros((1,), jnp.float32)}
    _L0_attn_in = _L0_attn_setup()

    def _L0_ffn_setup():
        import jax, jax.numpy as jnp
        import numpy as np
        D_IN, D_HID = (128, 512)

        def _ternary(key, shape):
            return jax.random.randint(key, shape, -1, 2).astype(jnp.float32)

        def _tlin(x, w, s):
            return jnp.einsum('bsi,oi->bso', x, w) * s
        key = jax.random.key(seed)
        ks = jax.random.split(key, 12)
        inv = lambda fan: 1.0 / np.sqrt(fan).astype(np.float32)
        return {'x': jax.random.normal(ks[0], (4, 256, D_IN), dtype=jnp.float32), 'w1_w': _ternary(ks[1], (D_HID, D_IN)), 'w1_s': jax.random.uniform(ks[2], (D_HID,), dtype=jnp.float32) * inv(D_IN), 'w2_w': _ternary(ks[3], (D_HID, D_IN)), 'w2_s': jax.random.uniform(ks[4], (D_HID,), dtype=jnp.float32) * inv(D_IN), 'h1_w': _ternary(ks[5], (D_HID, D_HID)), 'h1_s': jax.random.uniform(ks[6], (D_HID,), dtype=jnp.float32) * inv(D_HID), 'h2_w': _ternary(ks[7], (D_HID, D_HID)), 'h2_s': jax.random.uniform(ks[8], (D_HID,), dtype=jnp.float32) * inv(D_HID), 'w3_w': _ternary(ks[9], (D_IN, D_HID)), 'w3_s': jax.random.uniform(ks[10], (D_IN,), dtype=jnp.float32) * inv(D_HID)}
    _L0_ffn_in = _L0_ffn_setup()
    _L0_c = _w((lambda *s: np.random.randn(*s).astype(np.float32) * 0.05)(1, 128))
    _L0_wmod = _w((lambda *s: np.random.randn(*s).astype(np.float32) * 0.05)(128, 6 * 128) * 128 ** (-0.5))

    def _L1_attn_setup():
        import jax, jax.numpy as jnp
        import numpy as np
        B, N, D, H = (8, 128, 128, 16)
        HD = D // H
        SCALE = HD ** (-0.5)
        key = jax.random.key(seed)
        k1, k2, k3, k4, k5 = jax.random.split(key, 5)
        return {'x': jax.random.normal(k1, (B, N, D), dtype=jnp.float32), 'qkv_w': jax.random.normal(k2, (3 * D, D), dtype=jnp.float32) * 0.02, 'qkv_b': jax.random.normal(k3, (3 * D,), dtype=jnp.float32) * 0.02, 'fc_w': jax.random.normal(k4, (D, D), dtype=jnp.float32) * 0.02, 'fc_b': jax.random.normal(k5, (D,), dtype=jnp.float32) * 0.02}
    _L1_attn_in = _L1_attn_setup()

    def _L1_ffn_setup():
        import jax, jax.numpy as jnp
        import numpy as np
        EMBED = 128
        D_FF = 4 * EMBED
        N_EXPERTS = 8
        TOP_K = 2
        B, S = (2, 128)
        key = jax.random.key(seed)
        ks = jax.random.split(key, 10)
        sc_d = 1.0 / np.sqrt(EMBED)
        sc_h = 1.0 / np.sqrt(D_FF)
        return {'inputs': jax.random.normal(ks[0], (B, S, EMBED), jnp.float32), 'rw1': jax.random.normal(ks[1], (EMBED, D_FF), jnp.float32) * sc_d, 'rb1': jnp.zeros((D_FF,), jnp.float32), 'rw2': jax.random.normal(ks[2], (D_FF, N_EXPERTS), jnp.float32) * sc_h, 'rb2': jnp.zeros((N_EXPERTS,), jnp.float32), 'W1': jax.random.normal(ks[3], (N_EXPERTS, EMBED, D_FF), jnp.float32) * sc_d, 'b1': jnp.zeros((N_EXPERTS, D_FF), jnp.float32), 'W2': jax.random.normal(ks[4], (N_EXPERTS, D_FF, EMBED), jnp.float32) * sc_h, 'b2': jnp.zeros((N_EXPERTS, EMBED), jnp.float32)}
    _L1_ffn_in = _L1_ffn_setup()
    _L1_c = _w((lambda *s: np.random.randn(*s).astype(np.float32) * 0.05)(1, 128))
    _L1_wmod = _w((lambda *s: np.random.randn(*s).astype(np.float32) * 0.05)(128, 6 * 128) * 128 ** (-0.5))
    _d = {'L0_attn_hidden_states': _L0_attn_in['hidden_states'], 'L0_attn_q_w': _L0_attn_in['q_w'], 'L0_attn_k_w': _L0_attn_in['k_w'], 'L0_attn_v_w': _L0_attn_in['v_w'], 'L0_attn_o_w': _L0_attn_in['o_w'], 'L0_attn_dw_r': _L0_attn_in['dw_r'], 'L0_attn_pw_r': _L0_attn_in['pw_r'], 'L0_attn_dw_i': _L0_attn_in['dw_i'], 'L0_attn_pw_i': _L0_attn_in['pw_i'], 'L0_attn_gate_w': _L0_attn_in['gate_w'], 'L0_attn_alpha_raw': _L0_attn_in['alpha_raw'], 'L0_ffn_w1_w': _L0_ffn_in['w1_w'], 'L0_ffn_w1_s': _L0_ffn_in['w1_s'], 'L0_ffn_w2_w': _L0_ffn_in['w2_w'], 'L0_ffn_w2_s': _L0_ffn_in['w2_s'], 'L0_ffn_h1_w': _L0_ffn_in['h1_w'], 'L0_ffn_h1_s': _L0_ffn_in['h1_s'], 'L0_ffn_h2_w': _L0_ffn_in['h2_w'], 'L0_ffn_h2_s': _L0_ffn_in['h2_s'], 'L0_ffn_w3_w': _L0_ffn_in['w3_w'], 'L0_ffn_w3_s': _L0_ffn_in['w3_s'], 'L0_c': _L0_c, 'L0_wmod': _L0_wmod, 'L1_attn_qkv_w': _L1_attn_in['qkv_w'], 'L1_attn_qkv_b': _L1_attn_in['qkv_b'], 'L1_attn_fc_w': _L1_attn_in['fc_w'], 'L1_attn_fc_b': _L1_attn_in['fc_b'], 'L1_ffn_rw1': _L1_ffn_in['rw1'], 'L1_ffn_rb1': _L1_ffn_in['rb1'], 'L1_ffn_rw2': _L1_ffn_in['rw2'], 'L1_ffn_rb2': _L1_ffn_in['rb2'], 'L1_ffn_W1': _L1_ffn_in['W1'], 'L1_ffn_b1': _L1_ffn_in['b1'], 'L1_ffn_W2': _L1_ffn_in['W2'], 'L1_ffn_b2': _L1_ffn_in['b2'], 'L1_c': _L1_c, 'L1_wmod': _L1_wmod}
    _x0 = _d['L0_attn_hidden_states']
    _d['L0_attn_hidden_states'] = jax.random.normal(jax.random.fold_in(jax.random.key(seed), 1), (1, 2048, 128), dtype=_x0.dtype)
    del _x0
    return _d

def reference(L0_attn_hidden_states, L0_attn_q_w, L0_attn_k_w, L0_attn_v_w, L0_attn_o_w, L0_attn_dw_r, L0_attn_pw_r, L0_attn_dw_i, L0_attn_pw_i, L0_attn_gate_w, L0_attn_alpha_raw, L0_ffn_w1_w, L0_ffn_w1_s, L0_ffn_w2_w, L0_ffn_w2_s, L0_ffn_h1_w, L0_ffn_h1_s, L0_ffn_h2_w, L0_ffn_h2_s, L0_ffn_w3_w, L0_ffn_w3_s, L0_c, L0_wmod, L1_attn_qkv_w, L1_attn_qkv_b, L1_attn_fc_w, L1_attn_fc_b, L1_ffn_rw1, L1_ffn_rb1, L1_ffn_rw2, L1_ffn_rb2, L1_ffn_W1, L1_ffn_b1, L1_ffn_W2, L1_ffn_b2, L1_c, L1_wmod):

    def _L0_attn_ref(hidden_states, q_w, k_w, v_w, o_w, dw_r, pw_r, dw_i, pw_i, gate_w, alpha_raw):
        import jax, jax.numpy as jnp
        import numpy as np
        HID = 128
        NH = 16
        NKV = 4
        HD = 64
        C = 64
        RATIO = 0.125
        KS = 7

        def _block_causal_attention(x, qw, kw, vw, ow, k):
            B, nc, _, D = x.shape
            T = nc * k
            xf = x.reshape(B, T, D)
            q = (xf @ qw.T).reshape(B, T, NH, HD).transpose(0, 2, 1, 3)
            kk = (xf @ kw.T).reshape(B, T, NKV, HD).transpose(0, 2, 1, 3)
            v = (xf @ vw.T).reshape(B, T, NKV, HD).transpose(0, 2, 1, 3)
            rep = NH // NKV
            kk = jnp.repeat(kk, rep, axis=1)
            v = jnp.repeat(v, rep, axis=1)
            chunk_ids = jnp.arange(T) // k
            mask = chunk_ids[:, None] >= chunk_ids[None, :]
            scores = jnp.einsum('bhqd,bhkd->bhqk', q, kk) / np.float32(np.sqrt(HD))
            scores = jnp.where(mask[None, None], scores, jnp.finfo(scores.dtype).min)
            p = jax.nn.softmax(scores, axis=-1)
            o = jnp.einsum('bhqk,bhkd->bhqd', p, v)
            o = o.transpose(0, 2, 1, 3).reshape(B, T, NH * HD)
            return (o @ ow.T).reshape(B, nc, k, D)

        def _causal_conv(x, dw, pw):
            B, nc, L, D = x.shape
            xc = x.reshape(B * nc, L, D).transpose(0, 2, 1)
            xp = jnp.pad(xc, ((0, 0), (0, 0), (KS - 1, 0)))
            y = jax.lax.conv_general_dilated(xp, dw, window_strides=(1,), padding='VALID', dimension_numbers=('NCH', 'OIH', 'NCH'), feature_group_count=D)
            y = jax.nn.gelu(y, approximate=False)
            y = jnp.einsum('ncl,oc->nol', y, pw)
            return y.transpose(0, 2, 1).reshape(B, nc, L, D)

        def _forward(hidden_states, q_w, k_w, v_w, o_w, dw_r, pw_r, dw_i, pw_i, gate_w, alpha_raw):
            B, N, D = hidden_states.shape
            pad_len = -N % C
            x = jnp.pad(hidden_states, ((0, 0), (0, pad_len), (0, 0))) if pad_len else hidden_states
            nc = x.shape[1] // C
            chunks = x.reshape(B, nc, C, D)
            Xh = jnp.fft.rfft(chunks.astype(jnp.float32), axis=2)
            M = Xh.shape[2]
            k = max(1, int(M * RATIO))
            X_low, X_high = (Xh[:, :, :k, :], Xh[:, :, k:, :])
            A_r = _block_causal_attention(X_low.real, q_w, k_w, v_w, o_w, k)
            A_i = _block_causal_attention(X_low.imag, q_w, k_w, v_w, o_w, k)
            A_low = jax.lax.complex(A_r, A_i)
            H_r = _causal_conv(X_high.real, dw_r, pw_r)
            H_i = _causal_conv(X_high.imag, dw_i, pw_i)
            g = jax.nn.sigmoid(chunks.mean(axis=2) @ gate_w.T)[:, :, None, :]
            A_high = jax.lax.complex(H_r * g, H_i * g) + X_high
            alpha = jax.nn.sigmoid(alpha_raw)
            A_low_fused = alpha * A_low + (1.0 - alpha) * X_low
            Y_hat = jnp.concatenate([A_low_fused, A_high], axis=2)
            Y = jnp.fft.irfft(Y_hat, n=C, axis=2)
            return Y.reshape(B, -1, D)[:, :N, :].astype(hidden_states.dtype)
        return _forward(hidden_states, q_w, k_w, v_w, o_w, dw_r, pw_r, dw_i, pw_i, gate_w, alpha_raw)

    def _L0_ffn_ref(x, w1_w, w1_s, w2_w, w2_s, h1_w, h1_s, h2_w, h2_s, w3_w, w3_s):
        import jax, jax.numpy as jnp
        import numpy as np
        D_IN, D_HID = (128, 512)

        def _ternary(key, shape):
            return jax.random.randint(key, shape, -1, 2).astype(jnp.float32)

        def _tlin(x, w, s):
            return jnp.einsum('bsi,oi->bso', x, w) * s
        h = jax.nn.silu(_tlin(x, w1_w, w1_s)) * _tlin(x, w2_w, w2_s)
        h = jax.nn.gelu(_tlin(h, h1_w, h1_s), approximate=False)
        h = jax.nn.gelu(_tlin(h, h2_w, h2_s), approximate=False)
        return _tlin(h, w3_w, w3_s)

    def _L1_attn_ref(x, qkv_w, qkv_b, fc_w, fc_b):
        import jax, jax.numpy as jnp
        import numpy as np
        B, N, D, H = (8, 128, 128, 16)
        HD = D // H
        SCALE = HD ** (-0.5)
        b, n, d = x.shape
        qkv = (jnp.einsum('bnd,ed->bne', x, qkv_w) + qkv_b).reshape(b, n, H, 3 * HD)
        q, k, v = jnp.split(qkv, 3, axis=-1)
        q = q.transpose(0, 2, 1, 3)
        k = k.transpose(0, 2, 1, 3)
        v = v.transpose(0, 2, 1, 3)
        attn = jax.nn.softmax(jnp.einsum('bhqd,bhkd->bhqk', q, k) * SCALE, axis=-1)
        out = jnp.einsum('bhqk,bhkd->bhqd', attn, v)
        out = out.transpose(0, 2, 1, 3).reshape(b, n, d)
        return jnp.einsum('bnd,ed->bne', out, fc_w) + fc_b + x

    def _L1_ffn_ref(inputs, rw1, rb1, rw2, rb2, W1, b1, W2, b2):
        import jax, jax.numpy as jnp
        import numpy as np
        EMBED = 128
        D_FF = 4 * EMBED
        N_EXPERTS = 8
        TOP_K = 2
        B, S = (2, 128)
        Bb, Ss, D = inputs.shape
        T = Bb * Ss
        xf = inputs.reshape(T, D)
        score = jax.nn.relu(xf @ rw1 + rb1) @ rw2 + rb2
        _, topi = jax.lax.top_k(score, TOP_K)
        mask = jnp.zeros(score.shape, bool).at[jnp.arange(T)[:, None], topi].set(True)
        gate = jax.nn.softmax(jnp.where(mask, score, -jnp.inf), axis=-1)
        out = jnp.zeros_like(xf)
        for e in range(N_EXPERTS):
            h = jax.nn.relu(xf @ W1[e] + b1[e])
            y = h @ W2[e] + b2[e]
            out = out + gate[:, e:e + 1] * y
        return out.reshape(Bb, Ss, D)
    x = L0_attn_hidden_states
    mod = (_silu(L0_c) @ L0_wmod).reshape(L0_c.shape[0], 6, 1, -1)
    sa, ca, ga, sb, cb, gb = (mod[:, 0], mod[:, 1], mod[:, 2], mod[:, 3], mod[:, 4], mod[:, 5])
    ga = (2 * (ga >= 0) - 1) * jnp.maximum(jnp.abs(ga), 0.25)
    gb = (2 * (gb >= 0) - 1) * jnp.maximum(jnp.abs(gb), 0.25)
    h = _layernorm(x, axis=-1) * (1 + ca) + sa
    x = x + ga * _L0_attn_ref(h, L0_attn_q_w, L0_attn_k_w, L0_attn_v_w, L0_attn_o_w, L0_attn_dw_r, L0_attn_pw_r, L0_attn_dw_i, L0_attn_pw_i, L0_attn_gate_w, L0_attn_alpha_raw)
    h = _layernorm(x, axis=-1) * (1 + cb) + sb
    x = x + gb * _L0_ffn_ref(h, L0_ffn_w1_w, L0_ffn_w1_s, L0_ffn_w2_w, L0_ffn_w2_s, L0_ffn_h1_w, L0_ffn_h1_s, L0_ffn_h2_w, L0_ffn_h2_s, L0_ffn_w3_w, L0_ffn_w3_s)
    mod = (_silu(L1_c) @ L1_wmod).reshape(L1_c.shape[0], 6, 1, -1)
    sa, ca, ga, sb, cb, gb = (mod[:, 0], mod[:, 1], mod[:, 2], mod[:, 3], mod[:, 4], mod[:, 5])
    ga = (2 * (ga >= 0) - 1) * jnp.maximum(jnp.abs(ga), 0.25)
    gb = (2 * (gb >= 0) - 1) * jnp.maximum(jnp.abs(gb), 0.25)
    h = _layernorm(x, axis=-1) * (1 + ca) + sa
    x = x + ga * _L1_attn_ref(h, L1_attn_qkv_w, L1_attn_qkv_b, L1_attn_fc_w, L1_attn_fc_b)
    h = _layernorm(x, axis=-1) * (1 + cb) + sb
    x = x + gb * _L1_ffn_ref(h, L1_ffn_rw1, L1_ffn_rb1, L1_ffn_rw2, L1_ffn_rb2, L1_ffn_W1, L1_ffn_b1, L1_ffn_W2, L1_ffn_b2)
    return x

_drawn_inputs = setup_inputs


def setup_inputs(seed=0):
    import zlib

    import numpy as np

    out = dict(_drawn_inputs(seed))
    spreads = {'L1_ffn_rb1': (0.0, 0.1),
     'L1_ffn_rb2': (0.0, 0.1),
     'L1_ffn_b1': (0.0, 0.1),
     'L1_ffn_b2': (0.0, 0.1)}
    factors = {}
    for name, (base, spread) in spreads.items():
        noise = np.random.default_rng([zlib.crc32(name.encode()), seed]).standard_normal(out[name].shape)
        drawn = base * np.exp(spread * noise) if base else spread * noise
        out[name] = jnp.asarray(drawn.astype(out[name].dtype))
    for name, factor in factors.items():
        out[name] = (out[name] * factor).astype(out[name].dtype)
    return out
```

```python
from collections import namedtuple
from contextlib import ExitStack

import numpy as np

import concourse.bass as bass
from concourse import mybir

F32 = mybir.dt.float32
F32R = mybir.dt.float32r
BF16 = mybir.dt.bfloat16
ALU = mybir.AluOpType
ACT = mybir.ActivationFunctionType
AX = mybir.AxisListType.X

P = 128
TOK = 2048
NT = TOK // P
TB = TOK // 512
C = 64
NCH = TOK // C
M = C // 2 + 1
KL = 4
NH_ = M - KL
KS = 7
HEADS, KV, HD = 16, 4, 64
FF = 512
FB = FF // P
H1, D1 = 16, 8
G4 = 4
HG = H1 // G4
VW = 16
EXP = 8
SCALE1 = float(D1) ** -0.5
LEAD = 20

CONSTS = [("ident", 128), ("before", 64), ("ones", 128), ("lo_q", 1), ("lo_k", 1), ("one_rows", 1)]
MODS = [("c", 2), ("wmod0", 768), ("wmod1", 768), ("dft", 4 * M), ("idft", 128), ("mask_row", 128),
        ("mask_col", 512)]
SPECTRAL = [("qw", 1024), ("kw", 256), ("vw", 256), ("ow", 1024), ("dw_r", KS), ("dw_i", KS), ("pw_r", 128),
            ("pw_i", 128), ("gate_w", 128), ("alpha", 1)]
FFN = [("w1", 512), ("w2", 512), ("h1", 2048), ("h2", 2048), ("w3", 512), ("s1", 4), ("s2", 4), ("hs1", 4),
       ("hs2", 4), ("s3", 1)]
ATTN = [("kw1", 512), ("qw1", 512), ("vw1", H1 * VW), ("vb1", H1 * VW), ("kb1", HG), ("qb1", HG), ("fc", 128),
        ("fcb", 1)]
MOE = [("rw1", 512), ("rb1", 4), ("rw2", 32), ("rb2", 8), ("ew1", EXP * FF), ("eb1", EXP * FB),
       ("ew2", EXP * FF), ("eb2", 128)]


def width(pack):
    return sum(n for _, n in pack)


SEMS = """x_in consts_in mods_in spectral_in ffn_in attn_in moe_in silu_sig silu_ready mod_ready vec stats ln_var ln_std
ln_z zT_ready hT_ready diag_ready bcast_ready bcast_copied dft_ready spec_copied dc_ready qkv_ready q_copied
kv_copied kv_zero gate_ready g_ready alpha_ready pad_zero conv_step gelu_ready pw_ready pw_step y_ready
mask_ready s_ready s_max s_sub s_exp s_sum s_rcp p_ready pT_ready pT_copied o_ready o_copied aT_ready low_step
yT_ready yT_copied idft_ready x1_ready u_ready t_ready ug_ready a_ready h1_ready b_ready w3_ready w3_scaled
x2_ready kq_ready kq_hi kq_done v_ready v_copied qpad_zero qpad_filled nat_ready nat_max m_step mT_ready
mT_copied mrow_in st_ready exp_done pv_ready u_copied uT_ready u_rcp o_norm oT_ready oT_copied fc_ready
fc_copied yn_ready x3_ready rh_ready rh_copied sc_ready sc_copied scT_ready gt_step gtT_ready gtT_copied
b2_ready acc_step eh_ready eh_copied ey_ready acc_ready out_ready out_done aux_ready""".split()


def adaln_pair(nc, x_in, consts_in, mods_in, spectral_in, ffn_in, attn_in, moe_in, out):
    with ExitStack() as ctx:
        def sb(name, shape, dt=F32, where=ctx):
            return where.enter_context(nc.sbuf_tensor(name, shape, dt))

        sem = namedtuple("Semaphores", SEMS)(*[ctx.enter_context(nc.semaphore(n)) for n in SEMS])
        ps = ctx.enter_context(nc.psum_tensor("ps", [P, 8, 512], F32))

        x = sb("x", [P, NT, P])
        z = sb("z", [P, NT, P])
        hT = sb("hT", [P, TOK])
        CW = sb("CW", [P, width(CONSTS)])
        AW = sb("AW", [P, width(ATTN)])
        MW = sb("MW", [P, width(MOE)])
        st = sb("st", [P, NT, 6])
        mv = sb("mv", [P, NT, 2])
        ve = sb("ve", [P, NT])
        sd = sb("sd", [P, NT])
        rstd = sb("rstd", [P, NT])
        silu = sb("silu", [P, 2])
        modv = sb("modv", [P, 12])
        gsgn = sb("gsgn", [P, 4])
        gneg = sb("gneg", [P, 4])
        gabs = sb("gabs", [P, 4])
        gv = sb("gv", [P, 4])
        cv = sb("cv", [P, 4])
        dc = sb("dc", [P, 1])
        al = sb("al", [P, 1])
        alg = sb("alg", [P, 1])
        alx = sb("alx", [P, 1])
        w3g = sb("w3g", [P, 1])
        diag = sb("diag", [P, 2, P])
        gb = sb("gb", [P, 2, P])
        hs = sb("hs", [P, FB])
        ss = sb("ss", [P, FB])
        kb_lo = sb("kb_lo", [P, HG])
        qb_lo = sb("qb_lo", [P, HG])
        kb_one = sb("kb_one", [P, HG])
        fcbg = sb("fcbg", [P, 1])

        l0 = ExitStack()
        with l0:
            DW = sb("DW", [P, width(MODS)], where=l0)
            SW = sb("SW", [P, width(SPECTRAL)], where=l0)
            FW = sb("FW", [P, width(FFN)], where=l0)
            xhi = sb("xhi", [P, 2, NCH, KS - 1 + NH_], where=l0)
            xlo = sb("xlo", [P, 2, NCH, KL], where=l0)
            cacc = sb("cacc", [P, 2, NCH, NH_], where=l0)
            g_sb = sb("g_sb", [P, NCH], where=l0)
            Y = sb("Y", [P, NCH, C], where=l0)
            YT = sb("YT", [P, NT, P], where=l0)
            QT = sb("QT", [P, 8, 256], where=l0)
            Kp = sb("Kp", [P, 2, KV, P], where=l0)
            Vl = sb("Vl", [P, 2, 256], where=l0)
            mrow = sb("mrow", [32, P], BF16, where=l0)
            mcol = sb("mcol", [32, 512], BF16, where=l0)
            Pn = sb("Pn", [P, 2, G4, P], where=l0)
            PT = sb("PT", [P, 2, 512], where=l0)
            smax = sb("smax", [P, 2, G4], where=l0)
            ssum = sb("ssum", [P, 2, G4], where=l0)
            srcp = sb("srcp", [P, 2, G4], where=l0)
            OT = sb("OT", [P, 8, 2, P], where=l0)
            lowt = sb("lowt", [P, 2, NCH, KL], where=l0)
            tanh_t = sb("tanh_t", [P, 2, 512], where=l0)
            ug = sb("ug", [P, 2, 512], where=l0)
            act_a = Y[:, :, :].rearrange("p (f c) k -> p f (c k)", f=FB)
            act_b = YT[:, :, :].rearrange("p (f t) k -> p f (t k)", f=FB)
            act_c = sb("act_c", [P, FB, 512], where=l0)
            w3t = sb("w3t", [P, 4, P], where=l0)
        l1 = ExitStack()
        with l1:
            Ks = sb("Ks", [P, HG, TOK], F32R, where=l1)
            Qs = sb("Qs", [P, HG, TOK], F32R, where=l1)
            Qp = sb("Qp", [P, HG, G4, 512], F32R, where=l1)
            V = sb("V", [P, NT, H1 * VW], where=l1)
            hi = sb("hi", [P, 2, 512], F32R, where=l1)
            probs = sb("probs", [P, 8, 512], where=l1)
            mx = sb("mx", [P, 2, 16, 2], where=l1)
            mn = sb("mn", [P, 16], where=l1)
            m2 = sb("m2", [P, 4, 8], where=l1)
            mhi = sb("mhi", [P, 16], F32R, where=l1)
            mT = sb("mT", [8, 512], F32R, where=l1)
            U = sb("U", [P, 512], where=l1)
            rden = sb("rden", [P, 4, G4], where=l1)
        l2 = ExitStack()
        with l2:
            OnT = sb("OnT", [P, 2, 512], where=l2)
            yT = sb("yT", [P, 2, 512], where=l2)
            rh = sb("rh", [P, FB, 512], where=l2)
            eh = sb("eh", [P, 2, FB, 512], where=l2)
            scT = sb("scT", [8, 512], where=l2)
            sc = sb("sc", [P, 4, 8], where=l2)
            cmp = sb("cmp", [P, 4, 8, 8], where=l2)
            tie = sb("tie", [P, 4, 8, 8], where=l2)
            rank = sb("rank", [P, 4, 8], where=l2)
            top = sb("top", [P, 4], where=l2)
            gs = sb("gs", [P, 4], where=l2)
            gate = sb("gate", [P, 4, 8], where=l2)
            gtT = sb("gtT", [8, 512], where=l2)
            acc = sb("acc", [P, 4, P], where=l2)

        def columns(tensor, pack):
            at, views = 0, {}
            for name, n in pack:
                views[name] = tensor[:, at:at + n]
                at += n
            return views

        cw, dw_, sw, fw, aw, mw = (columns(t, p) for t, p in ((CW, CONSTS), (DW, MODS), (SW, SPECTRAL), (FW, FFN),
                                                              (AW, ATTN), (MW, MOE)))
        ident = cw["ident"]

        def wide(ap, shape, axis):
            return ap.unsqueeze(axis).broadcast_to(shape)

        def bank(n):
            return ps[:, n, :]

        def tiles4(ap):
            return ap.rearrange("p (t d) -> p t d", t=4)

        def cols(i, size):
            return slice(i * size, (i + 1) * size) if isinstance(i, int) else bass.ts(i, size)

        def due(count):
            return not isinstance(count, int) or count > 0

        def spectrum(b):
            return ps[:, b, 0:4 * 2 * M].rearrange("p (c r f) -> p r c f", r=2, f=M)

        groups = [(ri, j) for ri in range(2) for j in range(KV)]

        mod_cols = modv[:, :].rearrange("p (k three) -> p k three", three=3)
        shift, gate_raw = mod_cols[:, :, 0], mod_cols[:, :, 2]

        block_ = ctx.enter_context(nc.Block())

        @block_.sync
        def _(sp):
            x_tiles = x_in.rearrange("(t p) d -> p t d", p=P)
            for b in range(TB):
                sp.dma_start(x[:, 4 * b:4 * b + 4, :], x_tiles[:, 4 * b:4 * b + 4, :]).then_inc(sem.x_in, 16)
            sp.dma_start(CW[:, :], consts_in).then_inc(sem.consts_in, 16)
            sp.dma_start(FW[:, :], ffn_in).then_inc(sem.ffn_in, 16)
            sp.dma_start(AW[:, :], attn_in).then_inc(sem.attn_in, 16)
            sp.dma_start(MW[:, :], moe_in).then_inc(sem.moe_in, 16)
            def put_max(qb, hg):
                sp.wait_ge(sem.mT_copied, 4 * qb + hg + 1)
                for part in range(2):
                    for g in range(G4):
                        row = 32 * g + 24 + part
                        sp.dma_start(Qp[row:row + 1, hg, g, :].bitcast(F32),
                                     mT[4 * part + g:4 * part + g + 1, :].bitcast(F32)) \
                          .then_inc(sem.mrow_in, 16)
            with sp.Fori(0, TB) as qb:
                for hg in range(HG):
                    put_max(qb, hg)
            out_tiles = out.rearrange("(t p) d -> p t d", p=P)
            for b in range(TB):
                sp.wait_ge(sem.x3_ready, b + 1)
                sp.dma_start(out_tiles[:, 4 * b:4 * b + 4, :], x[:, 4 * b:4 * b + 4, :]).then_inc(sem.out_done, 16)
            sp.wait_ge(sem.out_done, 16 * TB)

        @block_.gpsimd
        def _(pool):
            pool.memset(xhi[:, :, :, 0:KS - 1], 0.0).then_inc(sem.pad_zero, 1)
            pool.memset(Kp[:, :, :, :], 0.0).then_inc(sem.kv_zero, 1)
            pool.wait_ge(sem.mods_in, 16)
            pool.tensor_copy(mrow[:, :], dw_["mask_row"][0:32, :]).then_inc(sem.mask_ready, 1)
            pool.tensor_copy(mcol[:, :], dw_["mask_col"][0:32, :]).then_inc(sem.mask_ready, 1)
            pool.wait_ge(sem.x2_ready, TB)
            pool.memset(Qp[:, :, :, :].bitcast(F32), 0.0).then_inc(sem.qpad_zero, 1)
            pool.wait_ge(sem.qpad_zero, 1)
            pool.wait_ge(sem.kq_done, 2 * HG * TB)

            def fill(qb, hg):
                if not (isinstance(qb, int) and qb == 0):
                    pool.wait_ge(sem.st_ready, 64 * (4 * (qb - 1) + hg + 1))
                for g in range(G4):
                    rows = slice(32 * g, 32 * g + 32)
                    pool.tensor_copy(Qp[rows, hg, g, :], Qs[rows, hg, cols(qb, 512)]) \
                        .then_inc(sem.qpad_filled, 1)

            for hg in range(HG):
                fill(0, hg)
            with pool.Fori(1, TB) as qb:
                for hg in range(HG):
                    fill(qb, hg)

        @block_.scalar
        def _(act):
            act.dma_start(DW[:, :], mods_in).then_inc(sem.mods_in, 16)
            act.dma_start(SW[:, :], spectral_in).then_inc(sem.spectral_in, 16)
            act.wait_ge(sem.mods_in, 16)
            act.activation(silu[:, :], dw_["c"], ACT.Sigmoid).then_inc(sem.silu_sig, 1)
            act.wait_ge(sem.spectral_in, 16)
            act.activation(al[:, :], sw["alpha"], ACT.Sigmoid).then_inc(sem.alpha_ready, 1)

            def ln_std(k):
                act.wait_ge(sem.ln_var, k + 1)
                act.activation(sd[:, :], ve[:, :], ACT.Sqrt).then_inc(sem.ln_std, 1)

            def ln_out(k):
                for b in range(TB):
                    act.wait_ge(sem.zT_ready, TB * (k - 1) + b + 1)
                    act.activation(hT[:, 512 * b:512 * b + 512], bank(1 + b), ACT.Identity,
                                   bias=modv[:, 3 * k:3 * k + 1], scale=cv[:, k:k + 1]).then_inc(sem.hT_ready, 1)

            ln_std(0)
            act.wait_ge(sem.vec, 11)
            act.wait_ge(sem.pad_zero, 1)
            for u in range(8):
                act.wait_ge(sem.dft_ready, u + 1)
                sp_ = spectrum(u % 4)
                act.activation(xhi[:, :, 4 * u:4 * u + 4, KS - 1:], sp_[:, :, :, KL:M], ACT.Identity,
                               scale=cv[:, 0:1]).then_inc(sem.spec_copied, 1)
                act.activation(xlo[:, :, 4 * u:4 * u + 4, :], sp_[:, :, :, 0:KL], ACT.Identity,
                               scale=cv[:, 0:1]).then_inc(sem.spec_copied, 1)
            for n in range(4):
                act.wait_ge(sem.qkv_ready, n + 1)
                act.activation(QT[:, 2 * n:2 * n + 2, :], bank(4 + n).rearrange("p (b n) -> p b n", b=2),
                               ACT.Copy).then_inc(sem.q_copied, 1)
            act.wait_ge(sem.qkv_ready, 5)
            act.wait_ge(sem.kv_zero, 1)
            for half in range(2):
                rows = slice(64 * half, 64 * half + 64)
                act.activation(Kp[rows, :, half::2, :],
                               ps[rows, 0, :].rearrange("p (j r n) -> p r j n", j=2, r=2), ACT.Copy) \
                   .then_inc(sem.kv_copied, 1)
            act.wait_ge(sem.qkv_ready, 6)
            act.activation(Vl[:, :, :], bank(1).rearrange("p (r n) -> p r n", r=2), ACT.Copy) \
               .then_inc(sem.kv_copied, 1)
            act.wait_ge(sem.qkv_ready, 7)
            act.activation(g_sb[:, :], ps[:, 2, 0:NCH], ACT.Sigmoid, scale=1.0 / C).then_inc(sem.g_ready, 1)
            for ri in range(2):
                act.wait_ge(sem.conv_step, 2 * KS - 1 + ri)
                act.activation(cacc[:, ri, :, :], cacc[:, ri, :, :], ACT.Gelu).then_inc(sem.gelu_ready, 1)

            def low_exp(i):
                act.wait_ge(sem.s_sub, i + 1)
                act.activation(Pn[:, i % 2, :, :], Pn[:, i % 2, :, :], ACT.Exp, scale=float(HD) ** -0.5) \
                   .then_inc(sem.s_exp, 1)

            low_exp(0)
            for i, (ri, j) in enumerate(groups):
                if i + 1 < len(groups):
                    low_exp(i + 1)
                act.wait_ge(sem.pT_ready, i + 1)
                act.activation(PT[:, i % 2, :], bank(2 + i % 2), ACT.Copy).then_inc(sem.pT_copied, 1)
                act.wait_ge(sem.o_ready, i + 1)
                rows = slice(64 * (j % 2), 64 * (j % 2) + 64)
                act.activation(OT[rows, 4 * (j // 2):4 * (j // 2) + 4, ri, :],
                               ps[rows, 2 + i % 2, :].rearrange("p (b n) -> p b n", b=4), ACT.Copy) \
                   .then_inc(sem.o_copied, 1)
            for b in range(4):
                act.wait_ge(sem.yT_ready, b + 1)
                act.activation(YT[:, 4 * b:4 * b + 4, :], tiles4(bank(1 + b)), ACT.Copy).then_inc(sem.yT_copied, 1)
            for n in range(2):
                act.wait_ge(sem.bcast_ready, 2)
                act.activation(gb[:, n, :], ps[:, 7, n * P:n * P + P], ACT.Copy).then_inc(sem.bcast_copied, 1)
            ln_std(1)
            ln_out(1)

            act.wait_ge(sem.ffn_in, 16)
            act.wait_ge(sem.vec, 19)

            def ffn(tb):
                for fb in range(FB):
                    act.wait_ge(sem.u_ready, 4 * tb + fb + 1)
                    act.activation(tanh_t[:, fb % 2, :], bank(fb % 2), ACT.Tanh, scale=hs[:, fb:fb + 1]) \
                       .then_inc(sem.t_ready, 1)
                for half, (to, scale) in enumerate(((act_b, "hs1"), (act_c, "hs2"))):
                    for ob in range(FB):
                        act.wait_ge(sem.h1_ready, 8 * tb + 4 * half + ob + 1)
                        act.activation(to[:, ob, :], bank(4 + ob % 2), ACT.Gelu, scale=fw[scale][:, ob:ob + 1]) \
                           .then_inc(sem.b_ready, 1)

            ffn(0)
            with act.Fori(1, TB) as tb:
                ffn(tb)

            ln_std(2)
            ln_out(2)
            act.wait_ge(sem.attn_in, 16)
            for n in range(2 * HG * TB):
                kq, hg = n // (HG * TB), n // TB % HG
                act.wait_ge(sem.kq_ready, n + 1)
                if due(n - 1):
                    act.wait_ge(sem.kq_done, n - 1)
                act.activation(hi[:, n % 2, :], bank(n % 4), ACT.Identity, bias=(kb_lo, qb_lo)[kq][:, hg:hg + 1],
                               scale=cw[("lo_k", "lo_q")[kq]]).then_inc(sem.kq_hi, 1)

            def exps(qb, s):
                if s % 16 == 1 and not (isinstance(qb, int) and qb == 0 and s < 16):
                    grp = 4 * qb + s // 16
                    act.wait_ge(sem.pv_ready, 16 * grp)
                    act.wait_ge(sem.o_norm, grp)
                    act.activation(U[:, :], bank(6), ACT.Copy).then_inc(sem.u_copied, 1)
                for g in range(G4):
                    n = 256 * qb + 4 * s + g
                    if g == 0:
                        if due(64 * qb + s - 1):
                            act.wait_ge(sem.pv_ready, 64 * qb + s - 1)
                    act.wait_ge(sem.st_ready, n + 1)
                    act.activation(probs[:, 4 * (s % 2) + g, :], bank(4 + g % 2), ACT.Exp, scale=SCALE1) \
                       .then_inc(sem.exp_done, 1)

            for s in range(4):
                exps(0, s)
            with act.Fori(0, TB - 1) as qb:
                for s in range(4, 68):
                    exps(qb, s)
            for s in range(4, 64):
                exps(TB - 1, s)
            act.wait_ge(sem.pv_ready, 256)
            act.wait_ge(sem.o_norm, 16)
            act.activation(U[:, :], bank(6), ACT.Copy).then_inc(sem.u_copied, 1)

            def fc_in(b):
                act.wait_ge(sem.oT_ready, b + 1)
                act.activation(OnT[:, b % 2, :], bank(b % 2), ACT.Copy).then_inc(sem.oT_copied, 1)

            fc_in(0)
            for b in range(TB):
                if b + 1 < TB:
                    fc_in(b + 1)
                act.wait_ge(sem.fc_ready, b + 1)
                if due(b - 1):
                    act.wait_ge(sem.yn_ready, b - 1)
                act.activation(yT[:, b % 2, :], bank(2 + b % 2), ACT.Identity, bias=fcbg[:, 0:1],
                               scale=gv[:, 2:3]).then_inc(sem.fc_copied, 1)
            ln_std(3)
            ln_out(3)

            act.wait_ge(sem.moe_in, 16)

            def moe(tb):
                for fb in range(FB):
                    act.wait_ge(sem.rh_ready, 4 * tb + fb + 1)
                    act.activation(rh[:, fb, :], bank(4 + fb % 2), ACT.Relu, bias=mw["rb1"][:, fb:fb + 1]) \
                       .then_inc(sem.rh_copied, 1)

                def hidden(e):
                    for fb in range(FB):
                        act.wait_ge(sem.eh_ready, 32 * tb + 4 * e + fb + 1)
                        col = e * FB + fb
                        act.activation(eh[:, e % 2, fb, :], bank(fb % 2), ACT.Relu,
                                       bias=mw["eb1"][:, col:col + 1]).then_inc(sem.eh_copied, 1)

                act.wait_ge(sem.sc_ready, tb + 1)
                act.activation(scT[:, :], ps[0:8, 6, :], ACT.Copy).then_inc(sem.sc_copied, 1)
                hidden(0)
                hidden(1)
                act.wait_ge(sem.gt_step, 13 * tb + 8)
                act.activation(gate[:, :, :], sc[:, :, :], ACT.Exp).then_inc(sem.gate_ready, 1)
                act.wait_ge(sem.gtT_ready, tb + 1)
                act.activation(gtT[:, :], ps[0:8, 6, :], ACT.Copy).then_inc(sem.gtT_copied, 1)
                for e in range(2, EXP):
                    hidden(e)

            moe(0)
            with act.Fori(1, TB) as tb:
                moe(tb)

        @block_.tensor
        def _(pe):
            pe.wait_ge(sem.mods_in, 16)
            pe.wait_ge(sem.silu_ready, 1)
            for layer in range(2):
                for k in range(6):
                    last = pe.matmul(ps[:, 7, 6 * layer + k:6 * layer + k + 1],
                                     dw_[f"wmod{layer}"][:, k * P:k * P + P], silu[:, layer:layer + 1],
                                     start=True, stop=True)
            last.then_inc(sem.mod_ready, 1)
            for u in range(8):
                pe.wait_ge(sem.ln_z, 1 + 2 * (u + 1))
                if u >= 4:
                    pe.wait_ge(sem.spec_copied, 2 * (u - 3))
                for i in range(2):
                    last = pe.matmul(ps[:, u % 4, i * 4 * M:(i + 1) * 4 * M], z[:, 2 * u + i, :], dw_["dft"],
                                     start=True, stop=True)
                last.then_inc(sem.dft_ready, 1)
            low_flat = xlo[:, :, :, :].rearrange("p r c k -> p (r c k)")
            pe.wait_ge(sem.spec_copied, 16)
            pe.wait_ge(sem.dc_ready, 1)
            pe.wait_ge(sem.spectral_in, 16)
            pe.wait_ge(sem.vec, 1)
            for n in range(4):
                for i in range(2):
                    b = 2 * n + i
                    last = pe.matmul(ps[:, 4 + n, 256 * i:256 * i + 256], sw["qw"][:, b * P:b * P + P], low_flat,
                                     start=True, stop=True)
                last.then_inc(sem.qkv_ready, 1)
            for j in range(2):
                last = pe.matmul(ps[:, 0, 256 * j:256 * j + 256], sw["kw"][:, j * P:j * P + P], low_flat,
                                 start=True, stop=True)
            last.then_inc(sem.qkv_ready, 1)
            for ri in range(2):
                last = pe.matmul(ps[:, 1, 256 * ri:256 * ri + 256], low_flat[:, ri * P:ri * P + P], sw["vw"],
                                 start=True, stop=True)
            last.then_inc(sem.qkv_ready, 1)
            pe.matmul(ps[:, 2, 0:NCH], sw["gate_w"], xlo[:, 0, :, 0], start=True, stop=True) \
              .then_inc(sem.qkv_ready, 1)
            pe.wait_ge(sem.q_copied, 4)
            for ri in range(2):
                pe.wait_ge(sem.gelu_ready, ri + 1)
                for half in range(2):
                    n = 2 * ri + half
                    pe.matmul(ps[:, 4 + n, 0:16 * NH_], sw[("pw_r", "pw_i")[ri]],
                              cacc[:, ri, 16 * half:16 * half + 16, :].rearrange("p c f -> p (c f)"),
                              start=True, stop=True).then_inc(sem.pw_ready, 1)
            pe.wait_ge(sem.kv_copied, 3)
            pe.wait_ge(sem.g_ready, 1)
            pe.wait_ge(sem.mask_ready, 2)
            pe.wait_ge(sem.consts_in, 16)

            def low_scores(i):
                ri, j = groups[i]
                if due(i - 1):
                    pe.wait_ge(sem.s_sub, i - 1)
                pe.matmul(bank(i % 2), mrow[:, :], mcol[:, :], start=True, stop=False, skip_group_check=True)
                for b in range(G4):
                    last = pe.matmul(ps[:, i % 2, b * P:b * P + P],
                                     QT[:, 4 * (j // 2) + b, ri * P:ri * P + P], Kp[:, ri, j, :],
                                     start=False, stop=(b == G4 - 1), skip_group_check=True)
                last.then_inc(sem.s_ready, 1)

            low_scores(0)
            low_scores(1)
            for i, (ri, j) in enumerate(groups):
                pe.wait_ge(sem.p_ready, i + 1)
                if due(i - 1):
                    pe.wait_ge(sem.o_copied, i - 1)
                for b in range(G4):
                    last = pe.transpose(ps[:, 2 + i % 2, b * P:b * P + P], Pn[:, i % 2, b, :], ident)
                last.then_inc(sem.pT_ready, 1)
                if i + 2 < len(groups):
                    low_scores(i + 2)
                pe.wait_ge(sem.pT_copied, i + 1)
                row = 64 * (j % 2)
                pe.matmul(ps[row:row + 64, 2 + i % 2, :], Vl[:, ri, 64 * j:64 * j + 64], PT[:, i % 2, :],
                          start=True, stop=True).then_inc(sem.o_ready, 1)
            pe.wait_ge(sem.o_copied, 8)
            for b in range(8):
                last = pe.matmul(ps[:, 0, 0:256], sw["ow"][:, b * P:b * P + P],
                                 OT[:, b, :, :].rearrange("p r n -> p (r n)"), start=(b == 0), stop=(b == 7))
            last.then_inc(sem.aT_ready, 1)
            pe.wait_ge(sem.y_ready, 6)
            for b in range(4):
                for i in range(4):
                    t = 4 * b + i
                    last = pe.transpose(ps[:, 1 + b, i * P:i * P + P],
                                        Y[:, 2 * t:2 * t + 2, :].rearrange("p c k -> p (c k)"), ident)
                last.then_inc(sem.yT_ready, 1)
            for b in range(4):
                pe.wait_ge(sem.yT_copied, b + 1)
                pe.matmul(bank((5 + b) % 8), dw_["idft"], YT[:, 4 * b:4 * b + 4, :].rearrange("p t d -> p (t d)"),
                          start=True, stop=True).then_inc(sem.idft_ready, 1)
            pe.wait_ge(sem.diag_ready, 1)
            pe.wait_ge(sem.x1_ready, TB)
            for n in range(2):
                pe.matmul(ps[:, 7, n * P:n * P + P], cw["ones"], diag[:, n, :], start=True, stop=True) \
                  .then_inc(sem.bcast_ready, 1)

            def z_transposes(k):
                for b in range(TB):
                    pe.wait_ge(sem.ln_z, 17 * k + 1 + 4 * (b + 1))
                    for i in range(4):
                        last = pe.transpose(ps[:, 1 + b, i * P:i * P + P], z[:, 4 * b + i, :], ident)
                    last.then_inc(sem.zT_ready, 1)
                pe.wait_ge(sem.hT_ready, TB * k)

            z_transposes(1)
            pe.wait_ge(sem.ffn_in, 16)
            pe.wait_ge(sem.bcast_copied, 2)

            def ffn(tb):
                rhs = hT[:, cols(tb, 512)]
                for fb in range(FB):
                    if due(4 * tb + fb - 1):
                        pe.wait_ge(sem.a_ready, 4 * tb + fb - 1)
                    pe.matmul(bank(fb % 2), fw["w1"][:, fb * P:fb * P + P], rhs, start=True, stop=True)
                    pe.matmul(bank(2 + fb % 2), fw["w2"][:, fb * P:fb * P + P], rhs, start=True, stop=True) \
                      .then_inc(sem.u_ready, 1)
                for half, (src, w, ready, at) in enumerate(((act_a, "h1", sem.a_ready, 4 * tb),
                                                            (act_b, "h2", sem.b_ready, 8 * tb))):
                    for ob in range(FB):
                        if due(8 * tb + 4 * half + ob - 1):
                            pe.wait_ge(sem.b_ready, 8 * tb + 4 * half + ob - 1)
                        for fb in range(FB):
                            if ob == 0:
                                pe.wait_ge(ready, at + fb + 1)
                            col = fb * FF + ob * P
                            last = pe.matmul(bank(4 + ob % 2), fw[w][:, col:col + P], src[:, fb, :],
                                             start=(fb == 0), stop=(fb == FB - 1))
                        last.then_inc(sem.h1_ready, 1)
                pe.wait_ge(sem.b_ready, 8 * tb + 8)
                if due(tb):
                    pe.wait_ge(sem.w3_scaled, tb)
                for qt in range(4):
                    for fb in range(FB):
                        last = pe.matmul(ps[:, 6, qt * P:qt * P + P], act_c[:, fb, qt * P:qt * P + P],
                                         fw["w3"][:, fb * P:fb * P + P], start=(fb == 0), stop=(fb == FB - 1))
                last.then_inc(sem.w3_ready, 1)

            ffn(0)
            with pe.Fori(1, TB) as tb:
                ffn(tb)

            z_transposes(2)
            pe.wait_ge(sem.attn_in, 16)
            for n in range(2 * HG * TB):
                kq, hg, tb = n // (HG * TB), n // TB % HG, n % TB
                if due(n - 3):
                    pe.wait_ge(sem.kq_done, n - 3)
                pe.matmul(bank(n % 4), aw[("kw1", "qw1")[kq]][:, hg * P:hg * P + P],
                          hT[:, tb * 512:tb * 512 + 512], start=True, stop=True).then_inc(sem.kq_ready, 1)
            for u in range(NT // 2):
                if due(u - 1):
                    pe.wait_ge(sem.v_copied, u - 1)
                for i in range(2):
                    t = 2 * u + i
                    last = pe.matmul(ps[:, 4 + u % 2, 256 * i:256 * i + 256], hT[:, t * P:t * P + P], aw["vw1"],
                                     start=True, stop=True)
                last.then_inc(sem.v_ready, 1)

            def nat(qb, k, c):
                hg, qt, g = k // 16 % 4, k % 16 // 4, k % 4
                item = 64 * qb + k
                if c == 0 and k % 16 == 0:
                    pe.wait_ge(sem.qpad_filled, 4 * (4 * qb + k // 16 + 1))
                if c % 2 == 0:
                    if due(2 * item + c // 2 - 1):
                        pe.wait_ge(sem.nat_max, 2 * item + c // 2 - 1)
                mm = pe.matmul(bank(c), Qp[:, hg, g, qt * P:qt * P + P], Ks[:, hg, c * 512:c * 512 + 512],
                               start=True, stop=True)
                if c % 2:
                    mm.then_inc(sem.nat_ready, 1)

            def max_rows(qb, grp):
                pe.wait_ge(sem.m_step, 4 * (4 * qb + grp + 1))
                if due(4 * qb + grp):
                    pe.wait_ge(sem.o_norm, 4 * qb + grp)
                for qt in range(4):
                    last = pe.transpose(ps[0:8, 7, qt * P:qt * P + P], m2[:, qt, :], ident)
                last.then_inc(sem.mT_ready, 1)

            def turn_outputs(qb, grp):
                pe.wait_ge(sem.u_copied, 4 * qb + grp)
                pe.wait_ge(sem.o_norm, 4 * qb + grp)
                pe.wait_ge(sem.mT_copied, 4 * qb + grp + 1 if not (isinstance(qb, int) and 4 * qb + grp == 16) else 16)
                for qt in range(4):
                    last = pe.transpose(ps[:, 7, qt * P:qt * P + P], U[:, qt * P:qt * P + P], ident)
                last.then_inc(sem.uT_ready, 1)

            def values(qb, s):
                hg, kt = s // 16 % 4, s % 16
                if kt == 0:
                    if due(4 * qb + s // 16):
                        pe.wait_ge(sem.u_copied, 4 * qb + s // 16)
                for g in range(G4):
                    pe.wait_ge(sem.exp_done, 256 * qb + 4 * s + g + 1)
                    col = (4 * hg + g) * VW
                    last = pe.matmul(ps[32 * g:32 * g + VW, 6, :], V[:, kt, col:col + VW],
                                     probs[:, 4 * (s % 2) + g, :], start=(kt == 0), stop=(kt == 15))
                last.then_inc(sem.pv_ready, 1)

            def step(qb, s):
                hg, kt = s // 16 % 4, s % 16
                last_block = isinstance(qb, int) and qb == TB - 1
                if kt == 0:
                    pe.wait_ge(sem.mrow_in, 128 * (4 * qb + s // 16 + 1))
                for g in range(G4):
                    if due(256 * qb + 4 * s + g - 1):
                        pe.wait_ge(sem.exp_done, 256 * qb + 4 * s + g - 1)
                    pe.matmul(bank(4 + g % 2), Ks[:, hg, kt * P:kt * P + P], Qp[:, hg, g, :],
                              start=True, stop=True).then_inc(sem.st_ready, 1)
                    if not (last_block and s + LEAD >= 64):
                        nat(qb, s + LEAD, g)
                if kt == 2 and not (isinstance(qb, int) and qb == 0 and s < 16):
                    turn_outputs(qb, s // 16)
                if kt == 13 and not (last_block and s // 16 == 3):
                    max_rows(qb, s // 16 + 1)
                if not (isinstance(qb, int) and qb == 0 and s == 0):
                    values(qb, s - 1)

            pe.wait_ge(sem.v_copied, 8)
            pe.wait_ge(sem.kq_done, 32)
            pe.wait_ge(sem.o_norm, 1)
            for k in range(LEAD):
                for c in range(4):
                    nat(0, k, c)
            max_rows(0, 0)
            for s in range(4):
                step(0, s)
            with pe.Fori(0, TB - 1) as qb:
                for s in range(4, 68):
                    step(qb, s)
            for s in range(4, 64):
                step(TB - 1, s)
            values(TB - 1, 63)
            turn_outputs(TB - 1, 4)

            def turn_heads(b):
                pe.wait_ge(sem.o_norm, 17)
                for i in range(4):
                    last = pe.transpose(ps[:, b % 2, i * P:i * P + P], z[:, 4 * b + i, :], ident)
                last.then_inc(sem.oT_ready, 1)

            turn_heads(0)
            for b in range(TB):
                if b + 1 < TB:
                    if due(b):
                        pe.wait_ge(sem.oT_copied, b)
                    turn_heads(b + 1)
                pe.wait_ge(sem.oT_copied, b + 1)
                if due(b - 1):
                    pe.wait_ge(sem.fc_copied, b - 1)
                pe.matmul(bank(2 + b % 2), aw["fc"], OnT[:, b % 2, :], start=True, stop=False)
                pe.matmul(bank(2 + b % 2), ident, hT[:, 512 * b:512 * b + 512], start=False, stop=True) \
                  .then_inc(sem.fc_ready, 1)
                pe.wait_ge(sem.fc_copied, b + 1)
                if due(b - 1):
                    pe.wait_ge(sem.aux_ready, b - 1)
                for i in range(4):
                    last = pe.transpose(ps[:, 4 + b % 2, i * P:i * P + P], yT[:, b % 2, i * P:i * P + P], ident)
                last.then_inc(sem.yn_ready, 1)
            z_transposes(3)
            pe.wait_ge(sem.moe_in, 16)

            def moe(tb):
                rhs = hT[:, cols(tb, 512)]
                for fb in range(FB):
                    if due(4 * tb + fb - 1):
                        pe.wait_ge(sem.rh_copied, 4 * tb + fb - 1)
                    pe.matmul(bank(4 + fb % 2), mw["rw1"][:, fb * P:fb * P + P], rhs, start=True, stop=True) \
                      .then_inc(sem.rh_ready, 1)
                if due(tb):
                    pe.wait_ge(sem.gtT_copied, tb)
                for fb in range(FB):
                    pe.wait_ge(sem.rh_copied, 4 * tb + fb + 1)
                    last = pe.matmul(ps[0:8, 6, :], mw["rw2"][:, fb * EXP:fb * EXP + EXP], rh[:, fb, :],
                                     start=(fb == 0), stop=(fb == FB - 1))
                last.then_inc(sem.sc_ready, 1)

                def up(e):
                    for fb in range(FB):
                        if due(32 * tb + 4 * e + fb - 1):
                            pe.wait_ge(sem.eh_copied, 32 * tb + 4 * e + fb - 1)
                        col = e * FF + fb * P
                        pe.matmul(bank(fb % 2), mw["ew1"][:, col:col + P], rhs, start=True, stop=True) \
                          .then_inc(sem.eh_ready, 1)

                def down(e):
                    pe.wait_ge(sem.eh_copied, 32 * tb + 4 * e + 4)
                    if due(4 * (8 * tb + e - 1)):
                        pe.wait_ge(sem.acc_step, 4 * (8 * tb + e - 1))
                    for qt in range(4):
                        for fb in range(FB):
                            col = e * FF + fb * P
                            last = pe.matmul(ps[:, 2 + e % 2, qt * P:qt * P + P],
                                             eh[:, e % 2, fb, qt * P:qt * P + P], mw["ew2"][:, col:col + P],
                                             start=(fb == 0), stop=(fb == FB - 1))
                    last.then_inc(sem.ey_ready, 1)

                up(0)
                pe.wait_ge(sem.sc_copied, tb + 1)
                for qt in range(4):
                    last = pe.matmul(ps[:, 6, qt * 8:qt * 8 + 8], scT[:, qt * P:qt * P + P], ident[0:8, 0:8],
                                     start=True, stop=True)
                last.then_inc(sem.scT_ready, 1)
                up(1)
                pe.wait_ge(sem.gt_step, 13 * tb + 13)
                for qt in range(4):
                    last = pe.transpose(ps[0:8, 6, qt * P:qt * P + P], gate[:, qt, :], ident)
                last.then_inc(sem.gtT_ready, 1)
                down(0)
                pe.wait_ge(sem.gtT_copied, tb + 1)
                for qt in range(4):
                    last = pe.matmul(ps[:, 7, qt * P:qt * P + P], gtT[:, qt * P:qt * P + P], mw["eb2"][0:8, :],
                                     start=True, stop=True)
                last.then_inc(sem.b2_ready, 1)
                for e in range(2, EXP):
                    up(e)
                    down(e - 1)
                down(EXP - 1)

            moe(0)
            with pe.Fori(1, TB) as tb:
                moe(tb)

        @block_.vector
        def _(dve):
            def ln(k):
                for t in range(NT):
                    dve.bn_stats(st[:, t, :], x[:, t, :]).then_inc(sem.stats, 1)
                dve.wait_ge(sem.stats, 32 * k + 16)
                for t in range(NT):
                    dve.bn_aggr(mv[:, t, :], st[:, t, :]).then_inc(sem.stats, 1)
                dve.wait_ge(sem.stats, 32 * k + 32)
                dve.tensor_scalar(ve[:, :], mv[:, :, 1], 1e-5, None, ALU.add).then_inc(sem.ln_var, 1)
                dve.wait_ge(sem.ln_std, k + 1)
                dve.reciprocal(rstd[:, :], sd[:, :]).then_inc(sem.ln_z, 1)
                dve.wait_ge(sem.ln_z, 17 * k + 1)
                for t in range(NT):
                    dve.tensor_scalar(z[:, t, :], x[:, t, :], mv[:, t, 0:1], rstd[:, t:t + 1],
                                      ALU.subtract, ALU.mult).then_inc(sem.ln_z, 1)

            dve.wait_ge(sem.mods_in, 16)
            dve.wait_ge(sem.silu_sig, 1)
            dve.tensor_tensor(silu[:, :], silu[:, :], dw_["c"], ALU.mult).then_inc(sem.silu_ready, 1)
            dve.wait_ge(sem.x_in, 64)
            ln(0)
            dve.wait_ge(sem.mod_ready, 1)
            dve.tensor_copy(modv[:, :], ps[:, 7, 0:12]).then_inc(sem.vec, 1)
            dve.wait_ge(sem.vec, 1)
            dve.tensor_scalar(cv[:, :], mod_cols[:, :, 1], 1.0, None, ALU.add).then_inc(sem.vec, 1)
            dve.wait_ge(sem.vec, 2)
            dve.tensor_scalar(gsgn[:, :], gate_raw, 0.0, 2.0, ALU.is_ge, ALU.mult).then_inc(sem.vec, 1)
            dve.wait_ge(sem.vec, 3)
            dve.tensor_scalar(gneg[:, :], gate_raw, -1.0, None, ALU.mult).then_inc(sem.vec, 1)
            dve.wait_ge(sem.vec, 4)
            dve.tensor_scalar(gsgn[:, :], gsgn[:, :], -1.0, None, ALU.add).then_inc(sem.vec, 1)
            dve.wait_ge(sem.vec, 5)
            dve.tensor_tensor(gabs[:, :], gate_raw, gneg[:, :], ALU.max).then_inc(sem.vec, 1)
            dve.wait_ge(sem.vec, 6)
            dve.tensor_scalar(gabs[:, :], gabs[:, :], 0.25, None, ALU.max).then_inc(sem.vec, 1)
            dve.wait_ge(sem.vec, 7)
            dve.tensor_tensor(gv[:, :], gsgn[:, :], gabs[:, :], ALU.mult).then_inc(sem.vec, 1)
            dve.wait_ge(sem.vec, 8)
            dve.tensor_scalar(dc[:, :], modv[:, 0:1], float(C), None, ALU.mult).then_inc(sem.vec, 1)
            dve.wait_ge(sem.vec, 9)
            dve.wait_ge(sem.alpha_ready, 1)
            dve.tensor_tensor(alg[:, :], al[:, :], gv[:, 0:1], ALU.mult).then_inc(sem.vec, 1)
            dve.wait_ge(sem.vec, 10)
            dve.tensor_tensor(alx[:, :], gv[:, 0:1], alg[:, :], ALU.subtract).then_inc(sem.vec, 1)
            dve.wait_ge(sem.vec, 11)
            dve.wait_ge(sem.spec_copied, 16)
            dve.tensor_scalar(xlo[:, 0, :, 0], xlo[:, 0, :, 0], dc[:, 0:1], None, ALU.add).then_inc(sem.dc_ready, 1)
            dve.wait_ge(sem.spectral_in, 16)
            for j in range(KS):
                for ri in range(2):
                    tap = sw[("dw_r", "dw_i")[ri]][:, j:j + 1]
                    src = xhi[:, ri, :, j:j + NH_]
                    if j == 0:
                        ins = dve.tensor_scalar(cacc[:, ri, :, :], src, tap, None, ALU.mult)
                    else:
                        dve.wait_ge(sem.conv_step, 2 * (j - 1) + ri + 1)
                        ins = dve.scalar_tensor_tensor(out=cacc[:, ri, :, :], in0=src, scalar=tap,
                                                       in1=cacc[:, ri, :, :], op0=ALU.mult, op1=ALU.add)
                    ins.then_inc(sem.conv_step, 1)

            def four(ap):
                return wide(ap, [P, G4, P], 2)

            def low_top(i):
                p = i % 2
                s4 = bank(p).rearrange("p (b n) -> p b n", b=G4)
                dve.wait_ge(sem.s_ready, i + 1)
                if due(i - 1):
                    dve.wait_ge(sem.pT_ready, i - 1)
                dve.tensor_reduce(smax[:, p, :], s4, AX, ALU.max).then_inc(sem.s_max, 1)
                dve.wait_ge(sem.s_max, i + 1)
                dve.tensor_tensor(Pn[:, p, :, :], s4, four(smax[:, p, :]), ALU.subtract).then_inc(sem.s_sub, 1)

            low_top(0)
            for i in range(len(groups)):
                p = i % 2
                if i + 1 < len(groups):
                    low_top(i + 1)
                dve.wait_ge(sem.s_exp, i + 1)
                dve.tensor_reduce(ssum[:, p, :], Pn[:, p, :, :], AX, ALU.add).then_inc(sem.s_sum, 1)
                dve.wait_ge(sem.s_sum, i + 1)
                dve.reciprocal(srcp[:, p, :], ssum[:, p, :]).then_inc(sem.s_rcp, 1)
                dve.wait_ge(sem.s_rcp, i + 1)
                dve.tensor_tensor(Pn[:, p, :, :], Pn[:, p, :, :], four(srcp[:, p, :]), ALU.mult) \
                   .then_inc(sem.p_ready, 1)

            dve.wait_ge(sem.g_ready, 1)
            for n in range(4):
                ri, c = n // 2, slice(16 * (n % 2), 16 * (n % 2) + 16)
                dve.wait_ge(sem.pw_ready, n + 1)
                tmp = cacc[:, ri, c, :]
                dve.scalar_tensor_tensor(
                    out=tmp, in0=ps[:, 4 + n, 0:16 * NH_].rearrange("p (c f) -> p c f", f=NH_), scalar=gv[:, 0:1],
                    in1=wide(g_sb[:, c], [P, 16, NH_], 2), op0=ALU.mult, op1=ALU.mult).then_inc(sem.pw_step, 1)
                dve.wait_ge(sem.pw_step, n + 1)
                keep = NH_ - ri
                to = M + KL - 1 if ri else KL
                dve.scalar_tensor_tensor(out=Y[:, c, to:to + keep], in0=xhi[:, ri, c, KS - 1:KS - 1 + keep],
                                         scalar=gv[:, 0:1], in1=tmp[:, :, 0:keep], op0=ALU.mult, op1=ALU.add) \
                   .then_inc(sem.y_ready, 1)
            dve.tensor_scalar(lowt[:, :, :, :], xlo[:, :, :, :], alx[:, 0:1], None, ALU.mult).then_inc(sem.low_step, 1)
            dve.wait_ge(sem.low_step, 1)
            dve.wait_ge(sem.aT_ready, 1)
            aT = ps[:, 0, 0:256].rearrange("p (r c k) -> p r c k", r=2, k=KL)
            for ri in range(2):
                dve.scalar_tensor_tensor(out=Y[:, :, M * ri:M * ri + KL - ri], in0=aT[:, ri, :, ri:KL],
                                         scalar=alg[:, 0:1], in1=lowt[:, ri, :, ri:KL], op0=ALU.mult, op1=ALU.add) \
                   .then_inc(sem.y_ready, 1)
            dve.wait_ge(sem.ffn_in, 16)
            dve.wait_ge(sem.attn_in, 16)
            dve.wait_ge(sem.consts_in, 16)
            dve.tensor_tensor(w3g[:, :], fw["s3"], gv[:, 1:2], ALU.mult).then_inc(sem.vec, 1)
            dve.wait_ge(sem.vec, 12)
            dve.tensor_scalar(diag[:, 0, :], ident, w3g[:, 0:1], None, ALU.mult).then_inc(sem.vec, 1)
            dve.wait_ge(sem.vec, 13)
            dve.tensor_scalar(diag[:, 1, :], ident, gv[:, 3:4], None, ALU.mult).then_inc(sem.diag_ready, 1)
            dve.wait_ge(sem.diag_ready, 1)
            dve.tensor_scalar(hs[:, :], fw["s1"], 0.5, None, ALU.mult).then_inc(sem.vec, 1)
            dve.wait_ge(sem.vec, 14)
            dve.tensor_tensor(ss[:, :], hs[:, :], fw["s2"], ALU.mult).then_inc(sem.vec, 1)
            dve.wait_ge(sem.vec, 15)
            dve.tensor_scalar(kb_lo[:, :], aw["kb1"], cw["lo_k"], None, ALU.mult).then_inc(sem.vec, 1)
            dve.wait_ge(sem.vec, 16)
            dve.tensor_scalar(qb_lo[:, :], aw["qb1"], cw["lo_q"], None, ALU.mult).then_inc(sem.vec, 1)
            dve.wait_ge(sem.vec, 17)
            dve.tensor_scalar(kb_one[:, :], aw["kb1"], cw["one_rows"], None, ALU.add).then_inc(sem.vec, 1)
            dve.wait_ge(sem.vec, 18)
            dve.tensor_tensor(fcbg[:, :], aw["fcb"], gv[:, 2:3], ALU.mult).then_inc(sem.vec, 1)
            dve.wait_ge(sem.vec, 19)
            for b in range(TB):
                dve.wait_ge(sem.idft_ready, b + 1)
                xt = x[:, 4 * b:4 * b + 4, :]
                dve.tensor_tensor(xt, tiles4(bank((5 + b) % 8)), xt, ALU.add).then_inc(sem.x1_ready, 1)
            dve.wait_ge(sem.x1_ready, TB)
            ln(1)
            dve.wait_ge(sem.bcast_copied, 2)

            def ffn(tb):
                for fb in range(FB):
                    n = 4 * tb + fb + 1
                    dve.wait_ge(sem.t_ready, n)
                    dve.scalar_tensor_tensor(out=ug[:, fb % 2, :], in0=tanh_t[:, fb % 2, :], scalar=1.0,
                                                       in1=bank(fb % 2), op0=ALU.add, op1=ALU.mult).then_inc(sem.ug_ready, 1)
                    dve.wait_ge(sem.ug_ready, n)
                    if fb == 0:
                        if due(8 * tb - 4):
                            dve.wait_ge(sem.h1_ready, 8 * tb - 4)
                    dve.scalar_tensor_tensor(out=act_a[:, fb, :], in0=ug[:, fb % 2, :], scalar=ss[:, fb:fb + 1],
                                             in1=bank(2 + fb % 2), op0=ALU.mult, op1=ALU.mult) \
                       .then_inc(sem.a_ready, 1)
                dve.wait_ge(sem.w3_ready, tb + 1)
                if due(tb):
                    dve.wait_ge(sem.x2_ready, tb)
                dve.tensor_tensor(w3t[:, :, :], tiles4(bank(6)), wide(gb[:, 0, :], [P, 4, P], 1),
                                            ALU.mult).then_inc(sem.w3_scaled, 1)
                dve.wait_ge(sem.w3_scaled, tb + 1)
                xt = x[:, cols(tb, 4), :]
                dve.tensor_tensor(xt, xt, w3t[:, :, :], ALU.add).then_inc(sem.x2_ready, 1)

            ffn(0)
            with dve.Fori(1, TB) as tb:
                ffn(tb)
            dve.wait_ge(sem.x2_ready, TB)
            ln(2)
            for n in range(2 * HG * TB):
                kq, hg, tb = n // (HG * TB), n // TB % HG, n % TB
                dve.wait_ge(sem.kq_hi, n + 1)
                dve.scalar_tensor_tensor(out=(Ks, Qs)[kq][:, hg, tb * 512:tb * 512 + 512], in0=bank(n % 4),
                                         scalar=(kb_one, aw["qb1"])[kq][:, hg:hg + 1], in1=hi[:, n % 2, :].bitcast(F32),
                                         op0=ALU.add, op1=ALU.subtract).then_inc(sem.kq_done, 1)
            for u in range(NT // 2):
                dve.wait_ge(sem.v_ready, u + 1)
                dve.tensor_tensor(V[:, 2 * u:2 * u + 2, :], bank(4 + u % 2).rearrange("p (t n) -> p t n", t=2),
                                  wide(aw["vb1"], [P, 2, H1 * VW], 1), ALU.add).then_inc(sem.v_copied, 1)
            dve.memset(bank(6), 0.0).then_inc(sem.o_norm, 1)

            def maxima(qb, k):
                for pair in range(2):
                    dve.wait_ge(sem.nat_ready, 2 * (64 * qb + k) + pair + 1)
                    dve.tensor_reduce(mx[:, k // 16 % 2, k % 16, pair:pair + 1],
                                      ps[:, 2 * pair:2 * pair + 2, :].rearrange("p b n -> p (b n)"), AX, ALU.max) \
                       .then_inc(sem.nat_max, 1)

            def minus_max(qb, grp):
                at = 4 * (4 * qb + grp)
                dve.wait_ge(sem.nat_max, 32 * (4 * qb + grp + 1))
                dve.tensor_reduce(mn[:, :], mx[:, grp % 2, :, :], AX, ALU.max).then_inc(sem.m_step, 1)
                dve.wait_ge(sem.m_step, at + 1)
                dve.tensor_scalar(mhi[:, :], mn[:, :], -1.0, None, ALU.mult).then_inc(sem.m_step, 1)
                dve.wait_ge(sem.m_step, at + 2)
                mn4 = mn[:, :].rearrange("p (q g) -> p q g", g=G4)
                dve.tensor_scalar(m2[:, :, 0:4], mn4, -1.0, None, ALU.mult).then_inc(sem.m_step, 1)
                dve.wait_ge(sem.m_step, at + 3)
                dve.scalar_tensor_tensor(out=m2[:, :, 4:8], in0=mn4, scalar=-1.0,
                                                   in1=mhi[:, :].bitcast(F32).rearrange("p (q g) -> p q g", g=G4),
                                                   op0=ALU.mult, op1=ALU.subtract).then_inc(sem.m_step, 1)
                dve.wait_ge(sem.m_step, at + 4)

            def copy_max_rows(qb, grp):
                dve.wait_ge(sem.mT_ready, 4 * qb + grp + 1)
                if due(128 * (4 * qb + grp)):
                    dve.wait_ge(sem.mrow_in, 128 * (4 * qb + grp))
                dve.tensor_copy(mT[:, :], ps[0:8, 7, :]).then_inc(sem.mT_copied, 1)

            def normalise(qb, grp):
                done = 4 * qb + grp
                dve.wait_ge(sem.uT_ready, done)
                turned = bank(7).rearrange("p (q g w) -> p q g w", q=4, g=G4)
                dve.reciprocal(rden[:, :, :], turned[:, :, :, D1]).then_inc(sem.u_rcp, 1)
                dve.wait_ge(sem.u_rcp, done)
                hg = (grp - 1) % 4
                to = z[:, cols(qb, 4), hg * 32:hg * 32 + 32].rearrange("p q (g w) -> p q g w", w=D1)
                dve.tensor_tensor(to, turned[:, :, :, 0:D1], wide(rden[:, :, :], [P, 4, G4, D1], 3), ALU.mult) \
                   .then_inc(sem.o_norm, 1)

            def step(qb, s):
                kt, grp = s % 16, s // 16
                last_block = isinstance(qb, int) and qb == TB - 1
                if not (last_block and s + LEAD >= 64):
                    maxima(qb, s + LEAD)
                if kt == 2 and not (isinstance(qb, int) and qb == 0 and s < 16):
                    normalise(qb, grp)
                if kt == 11 and not (last_block and grp == 3):
                    minus_max(qb, grp + 1)
                if kt == 13 and not (last_block and grp == 3):
                    copy_max_rows(qb, grp + 1)

            for k in range(16):
                maxima(0, k)
            minus_max(0, 0)
            for k in range(16, LEAD):
                maxima(0, k)
            copy_max_rows(0, 0)
            for s in range(4):
                step(0, s)
            with dve.Fori(0, TB - 1) as qb:
                for s in range(4, 68):
                    step(qb, s)
            for s in range(4, 64):
                step(TB - 1, s)
            normalise(TB - 1, 4)

            for b in range(TB):
                dve.wait_ge(sem.yn_ready, b + 1)
                xt = x[:, 4 * b:4 * b + 4, :]
                dve.tensor_tensor(xt, tiles4(bank(4 + b % 2)), xt, ALU.add).then_inc(sem.aux_ready, 1)
            dve.wait_ge(sem.aux_ready, TB)
            ln(3)

            def moe(tb):
                ranks = [P, 4, EXP, EXP]
                dve.wait_ge(sem.scT_ready, tb + 1)
                dve.tensor_tensor(sc[:, :, :], ps[:, 6, 0:32].rearrange("p (q e) -> p q e", e=EXP),
                                    wide(mw["rb2"], [P, 4, EXP], 1), ALU.add).then_inc(sem.gt_step, 1)
                dve.wait_ge(sem.gt_step, 13 * tb + 1)
                other, own = wide(sc[:, :, :], ranks, 2), wide(sc[:, :, :], ranks, 3)
                dve.tensor_tensor(cmp[:, :, :, :], other, own, ALU.is_gt).then_inc(sem.gt_step, 1)
                dve.wait_ge(sem.gt_step, 13 * tb + 2)
                dve.tensor_tensor(tie[:, :, :, :], other, own, ALU.is_equal).then_inc(sem.gt_step, 1)
                dve.wait_ge(sem.gt_step, 13 * tb + 3)
                before = wide(cw["before"].rearrange("p (e j) -> p e j", e=EXP), ranks, 1)
                dve.tensor_tensor(tie[:, :, :, :], tie[:, :, :, :], before, ALU.mult).then_inc(sem.gt_step, 1)
                dve.wait_ge(sem.gt_step, 13 * tb + 4)
                dve.tensor_tensor(cmp[:, :, :, :], cmp[:, :, :, :], tie[:, :, :, :], ALU.add).then_inc(sem.gt_step, 1)
                dve.wait_ge(sem.gt_step, 13 * tb + 5)
                dve.tensor_reduce(rank[:, :, :], cmp[:, :, :, :], AX, ALU.add).then_inc(sem.gt_step, 1)
                dve.wait_ge(sem.gt_step, 13 * tb + 6)
                dve.tensor_reduce(top[:, :], sc[:, :, :], AX, ALU.max).then_inc(sem.gt_step, 1)
                dve.wait_ge(sem.gt_step, 13 * tb + 7)
                dve.tensor_tensor(sc[:, :, :], sc[:, :, :], wide(top[:, :], [P, 4, EXP], 2), ALU.subtract).then_inc(sem.gt_step, 1)
                dve.wait_ge(sem.gt_step, 13 * tb + 8)
                dve.tensor_scalar(rank[:, :, :], rank[:, :, :], 2.0, None, ALU.is_lt).then_inc(sem.gt_step, 1)
                dve.wait_ge(sem.gt_step, 13 * tb + 9)
                dve.wait_ge(sem.gate_ready, tb + 1)
                dve.tensor_tensor(gate[:, :, :], gate[:, :, :], rank[:, :, :], ALU.mult).then_inc(sem.gt_step, 1)
                dve.wait_ge(sem.gt_step, 13 * tb + 10)
                dve.tensor_reduce(gs[:, :], gate[:, :, :], AX, ALU.add).then_inc(sem.gt_step, 1)
                dve.wait_ge(sem.gt_step, 13 * tb + 11)
                dve.reciprocal(gs[:, :], gs[:, :]).then_inc(sem.gt_step, 1)
                dve.wait_ge(sem.gt_step, 13 * tb + 12)
                dve.tensor_tensor(gate[:, :, :], gate[:, :, :], wide(gs[:, :], [P, 4, EXP], 2), ALU.mult).then_inc(sem.gt_step, 1)
                dve.wait_ge(sem.gt_step, 13 * tb + 13)
                dve.wait_ge(sem.b2_ready, tb + 1)
                dve.tensor_copy(acc[:, :, :], tiles4(bank(7))).then_inc(sem.acc_ready, 1)
                for e in range(EXP):
                    dve.wait_ge(sem.ey_ready, 8 * tb + e + 1)
                    if e == 0:
                        dve.wait_ge(sem.acc_ready, tb + 1)
                    else:
                        dve.wait_ge(sem.acc_step, 4 * (8 * tb + e))
                    for qt in range(4):
                        dve.scalar_tensor_tensor(out=acc[:, qt, :], in0=ps[:, 2 + e % 2, qt * P:qt * P + P],
                                                 scalar=gate[:, qt, e:e + 1], in1=acc[:, qt, :],
                                                 op0=ALU.mult, op1=ALU.add).then_inc(sem.acc_step, 1)
                dve.wait_ge(sem.acc_step, 4 * (8 * tb + 8))
                dve.tensor_tensor(acc[:, :, :], acc[:, :, :], wide(gb[:, 1, :], [P, 4, P], 1), ALU.mult).then_inc(sem.out_ready, 1)
                dve.wait_ge(sem.out_ready, tb + 1)
                xt = x[:, cols(tb, 4), :]
                dve.tensor_tensor(xt, xt, acc[:, :, :], ALU.add).then_inc(sem.x3_ready, 1)
                dve.wait_ge(sem.x3_ready, tb + 1)

            moe(0)
            with dve.Fori(1, TB) as tb:
                moe(tb)


def _pack(pack, parts):
    cols = []
    for name, n in pack:
        a = np.asarray(parts[name], np.float32)
        full = np.zeros((P, n), np.float32)
        full[:a.shape[0], :] = a
        cols.append(full)
    return np.ascontiguousarray(np.concatenate(cols, 1))


def _constants():
    n, f = np.arange(C)[:, None], np.arange(M)[None, :]
    angle = 2 * np.pi * ((n * f) % C) / C
    forward = np.concatenate([np.cos(angle), -np.sin(angle)], 1)
    weight = np.where((f == 0) | (f == M - 1), 1.0, 2.0) / C
    back = np.concatenate([np.cos(angle) * weight, (-np.sin(angle) * weight)[:, 1:M - 1]], 1).T
    dft, idft = np.zeros((P, 4 * M)), np.zeros((P, P))
    for c in range(2):
        dft[c * C:c * C + C, c * 2 * M:(c + 1) * 2 * M] = forward
        idft[c * C:c * C + C, c * C:c * C + C] = back
    blocks, token = np.arange(NCH)[:, None], np.arange(P)[None, :] // KL
    row = np.arange(P) % 32 // D1
    return {
        "dft": dft, "idft": idft, "ident": np.eye(P), "ones": np.ones((P, P)),
        "mask_row": (token == blocks), "mask_col": np.tile(np.where(token > blocks, -1e30, 0.0), (1, 4)),
        "before": np.tile(np.tril(np.ones((EXP, EXP)), -1).reshape(1, -1), (P, 1)),
        "lo_q": (row == 1)[:, None], "lo_k": (row == 2)[:, None],
        "one_rows": ((np.arange(P) % 32 == 24) | (np.arange(P) % 32 == 25))[:, None],
    }


def _columns(a):
    return a.reshape(-1, P).T


def _blocks(a):
    return a.reshape(-1, P, a.shape[-1]).transpose(1, 0, 2).reshape(P, -1)


def _stack(w):
    out = np.zeros((HG, G4, 32) + w.shape[2:], np.float32)
    for part in range(3):
        out[:, :, part * D1:(part + 1) * D1] = w.reshape((HG, G4) + w.shape[1:])
    return out.reshape((HG, P) + w.shape[2:])


def kernel(**inputs):
    import concourse.bacc as _bacc
    from concourse import mybir as _mybir
    from concourse.bass_utils import run_bass_kernel_spmd as _run

    i = {k: np.asarray(v) for k, v in inputs.items()}
    consts = _constants()
    q = i["L0_attn_q_w"].reshape(2, 2, G4, HD, P).transpose(0, 2, 1, 3, 4).reshape(HEADS * HD, P)
    o = i["L0_attn_o_w"].reshape(P, 2, 2, G4, HD).transpose(1, 3, 2, 4, 0).reshape(HEADS * HD, P)
    mods = dict(consts, c=np.concatenate([i["L0_c"], i["L1_c"]], 0).T, wmod0=i["L0_wmod"], wmod1=i["L1_wmod"])
    spectral = {
        "qw": q.T, "kw": i["L0_attn_k_w"].T, "vw": i["L0_attn_v_w"].T, "ow": _blocks(o),
        "dw_r": i["L0_attn_dw_r"][:, 0], "dw_i": i["L0_attn_dw_i"][:, 0], "pw_r": i["L0_attn_pw_r"].T,
        "pw_i": i["L0_attn_pw_i"].T, "gate_w": i["L0_attn_gate_w"].T,
        "alpha": np.broadcast_to(i["L0_attn_alpha_raw"][None], (P, 1)),
    }
    ffn = {
        "w1": i["L0_ffn_w1_w"].T, "w2": i["L0_ffn_w2_w"].T, "h1": _blocks(i["L0_ffn_h1_w"].T),
        "h2": _blocks(i["L0_ffn_h2_w"].T), "w3": _blocks(i["L0_ffn_w3_w"].T), "s1": _columns(i["L0_ffn_w1_s"]),
        "s2": _columns(i["L0_ffn_w2_s"]), "hs1": _columns(i["L0_ffn_h1_s"]), "hs2": _columns(i["L0_ffn_h2_s"]),
        "s3": _columns(i["L0_ffn_w3_s"]),
    }
    qkv = i["L1_attn_qkv_w"].reshape(H1, 3, D1, P)
    qkv_b = i["L1_attn_qkv_b"].reshape(H1, 3, D1)
    vw = np.zeros((P, H1, VW), np.float32)
    vb = np.zeros((P, H1, VW), np.float32)
    vw[:, :, 0:D1] = qkv[:, 2].transpose(2, 0, 1)
    vb[:, :, 0:D1] = qkv_b[:, 2]
    vb[:, :, D1] = 1.0
    attn = {
        "kw1": _stack(qkv[:, 1]).transpose(2, 0, 1).reshape(P, -1),
        "qw1": _stack(qkv[:, 0]).transpose(2, 0, 1).reshape(P, -1),
        "vw1": vw.reshape(P, -1), "vb1": vb.reshape(P, -1), "kb1": _stack(qkv_b[:, 1]).T,
        "qb1": _stack(qkv_b[:, 0]).T, "fc": i["L1_attn_fc_w"].T, "fcb": _columns(i["L1_attn_fc_b"]),
    }
    moe = {
        "rw1": i["L1_ffn_rw1"], "rb1": _columns(i["L1_ffn_rb1"]), "rw2": _blocks(i["L1_ffn_rw2"]),
        "rb2": np.broadcast_to(i["L1_ffn_rb2"][None], (P, EXP)),
        "ew1": i["L1_ffn_W1"].transpose(1, 0, 2).reshape(P, -1), "eb1": _columns(i["L1_ffn_b1"].reshape(-1)),
        "ew2": _blocks(i["L1_ffn_W2"].reshape(EXP * FF, P)), "eb2": i["L1_ffn_b2"],
    }
    arrays = {
        "x_in": np.ascontiguousarray(i["L0_attn_hidden_states"].reshape(TOK, P)),
        "consts_in": _pack(CONSTS, consts), "mods_in": _pack(MODS, mods), "spectral_in": _pack(SPECTRAL, spectral),
        "ffn_in": _pack(FFN, ffn), "attn_in": _pack(ATTN, attn), "moe_in": _pack(MOE, moe),
    }
    nc = _bacc.Bacc("TRN2", target_bir_lowering=False, num_devices=1)
    args = [nc.dram_tensor(n, a.shape, _mybir.dt.from_np(a.dtype), kind="ExternalInput").ap()
            for n, a in arrays.items()]
    out = nc.dram_tensor("out", (TOK, P), _mybir.dt.float32, kind="ExternalOutput").ap()
    adaln_pair(nc, *args, out)
    r = _run(nc, [arrays], core_ids=[0])
    return np.asarray(r.results[0]["out"]).reshape(1, TOK, P)
```

```python
from collections import namedtuple
from contextlib import ExitStack

import numpy as np

import concourse.bass as bass
from concourse import mybir

F32 = mybir.dt.float32
F32R = mybir.dt.float32r
BF16 = mybir.dt.bfloat16
ALU = mybir.AluOpType
ACT = mybir.ActivationFunctionType
AX = mybir.AxisListType.X

P = 128
TOK = 2048
NT = TOK // P
TB = TOK // 512
C = 64
NCH = TOK // C
M = C // 2 + 1
KL = 4
NH_ = M - KL
KS = 7
HEADS, KV, HD = 16, 4, 64
FF = 512
FB = FF // P
H1, D1 = 16, 8
G4 = 4
HG = H1 // G4
VW = 16
EXP = 8
SCALE1 = float(D1) ** -0.5
LEAD = 20

CONSTS = [("ident", 128), ("before", 64), ("ones", 128), ("lo_q", 1), ("lo_k", 1), ("one_rows", 1)]
MODS = [("c", 2), ("wmod0", 768), ("wmod1", 768), ("dft", 4 * M), ("idft", 128), ("mask_row", 128),
        ("mask_col", 512)]
SPECTRAL = [("qw", 1024), ("kw", 256), ("vw", 256), ("ow", 1024), ("dw_r", KS), ("dw_i", KS), ("pw_r", 128),
            ("pw_i", 128), ("gate_w", 128), ("alpha", 1)]
FFN = [("w1", 512), ("w2", 512), ("h1", 2048), ("h2", 2048), ("w3", 512), ("s1", 4), ("s2", 4), ("hs1", 4),
       ("hs2", 4), ("s3", 1)]
ATTN = [("kw1", 512), ("qw1", 512), ("vw1", H1 * VW), ("vb1", H1 * VW), ("kb1", HG), ("qb1", HG), ("fc", 128),
        ("fcb", 1)]
MOE = [("rw1", 512), ("rb1", 4), ("rw2", 32), ("rb2", 8), ("ew1", EXP * FF), ("eb1", EXP * FB),
       ("ew2", EXP * FF), ("eb2", 128)]


def width(pack):
    return sum(n for _, n in pack)


SEMS = """x_in consts_in mods_in spectral_in ffn_in attn_in moe_in silu_sig silu_ready mod_ready vec stats ln_var ln_std
ln_z zT_ready hT_ready hT_first hT_second w_first w_second w2_split e_first e_second af_ready ah_ready bh_ready bf_ready hb_free diag_ready bcast_ready bcast_copied dft_ready spec_copied dc_ready qkv_ready q_copied
kv_copied kv_zero gate_ready g_ready alpha_ready pad_zero conv_step gelu_ready pw_ready pw_step y_ready
mask_ready s_ready s_max s_sub s_exp s_sum s_rcp p_ready pT_ready pT_copied o_ready o_copied aT_ready low_step
yT_ready yT_copied idft_ready x1_ready u_ready t_ready ug_ready a_ready h_ready b_ready w3_ready w3_scaled
x2_ready kq_ready kq_hi kq_done v_ready v_copied qpad_zero qpad_filled nat_ready nat_max m_step mT_ready
mT_copied first_filled mrow_in st_ready exp_done pv_ready u_copied uT_ready u_rcp o_norm oT_ready oT_copied fc_ready
fc_copied yn_ready x3_ready rh_ready rh_copied sc_ready sc_copied scT_ready gt_step gtT_ready gtT_copied
b2_ready acc_step eh_ready eh_copied ey_ready acc_ready out_ready out_done aux_ready""".split()


def adaln_pair(nc, x_in, consts_in, mods_in, spectral_in, ffn_in, attn_in, moe_in, out):
    with ExitStack() as ctx:
        def sb(name, shape, dt=F32, where=ctx):
            return where.enter_context(nc.sbuf_tensor(name, shape, dt))

        sem = namedtuple("Semaphores", SEMS)(*[ctx.enter_context(nc.semaphore(n)) for n in SEMS])
        ps = ctx.enter_context(nc.psum_tensor("ps", [P, 8, 512], F32))

        x = sb("x", [P, NT, P])
        z = sb("z", [P, NT, P])
        hT = sb("hT", [P, TOK])
        CW = sb("CW", [P, width(CONSTS)])
        AW = sb("AW", [P, width(ATTN)])
        MW = sb("MW", [P, width(MOE)])
        st = sb("st", [P, NT, 6])
        mv = sb("mv", [P, NT, 2])
        ve = sb("ve", [P, NT])
        sd = sb("sd", [P, NT])
        rstd = sb("rstd", [P, NT])
        silu = sb("silu", [P, 2])
        modv = sb("modv", [P, 12])
        gsgn = sb("gsgn", [P, 4])
        gneg = sb("gneg", [P, 4])
        gabs = sb("gabs", [P, 4])
        gv = sb("gv", [P, 4])
        cv = sb("cv", [P, 4])
        dc = sb("dc", [P, 1])
        al = sb("al", [P, 1])
        alg = sb("alg", [P, 1])
        alx = sb("alx", [P, 1])
        w3g = sb("w3g", [P, 1])
        diag = sb("diag", [P, 2, P])
        gb = sb("gb", [P, 2, P])
        hs = sb("hs", [P, FB])
        ss = sb("ss", [P, FB])
        kb_lo = sb("kb_lo", [P, HG])
        qb_lo = sb("qb_lo", [P, HG])
        kb_one = sb("kb_one", [P, HG])
        fcbg = sb("fcbg", [P, 1])

        l0 = ExitStack()
        with l0:
            FW = sb("FW", [P, width(FFN)], where=l0)
            spectral = ExitStack()
            with spectral:
                DW = sb("DW", [P, width(MODS)], where=spectral)
                SW = sb("SW", [P, width(SPECTRAL)], where=spectral)
                xhi = sb("xhi", [P, 2, NCH, KS - 1 + NH_], where=spectral)
                xlo = sb("xlo", [P, 2, NCH, KL], where=spectral)
                cacc = sb("cacc", [P, 2, NCH, NH_], where=spectral)
                g_sb = sb("g_sb", [P, NCH], where=spectral)
                Y = sb("Y", [P, NCH, C], where=spectral)
                YT = sb("YT", [P, NT, P], where=spectral)
                QT = sb("QT", [P, 8, 256], where=spectral)
                Kp = sb("Kp", [P, 2, KV, P], where=spectral)
                Vl = sb("Vl", [P, 2, 256], where=spectral)
                mrow = sb("mrow", [32, P], BF16, where=spectral)
                mcol = sb("mcol", [32, 512], BF16, where=spectral)
                Pn = sb("Pn", [P, 2, G4, P], where=spectral)
                PT = sb("PT", [P, 2, 512], where=spectral)
                smax = sb("smax", [P, 2, G4], where=spectral)
                ssum = sb("ssum", [P, 2, G4], where=spectral)
                srcp = sb("srcp", [P, 2, G4], where=spectral)
                OT = sb("OT", [P, 8, 2, P], where=spectral)
                lowt = sb("lowt", [P, 2, NCH, KL], where=spectral)
            hT0 = [sb(f"hT0_{i}", [P, TOK], F32R, where=l0) for i in range(2)]
            w1_ = [sb(f"w1_{i}", [P, 2, FF], F32R, where=l0) for i in range(2)]
            h1_ = [sb(f"h1_{i}", [P, FB * FF], F32R, where=l0) for i in range(2)]
            h2_ = [sb(f"h2_{i}", [P, FB * FF], F32R, where=l0) for i in range(2)]
            tanh_t = sb("tanh_t", [P, 2, 512], where=l0)
            ug = sb("ug", [P, 2, 512], where=l0)
            af = sb("af", [P, 2, 512], where=l0)
            bf = sb("bf", [P, 2, 512], where=l0)
            act_a = [sb(f"act_a{i}", [P, FB, 512], F32R, where=l0) for i in range(2)]
            act_b = [sb(f"act_b{i}", [P, FB, 512], F32R, where=l0) for i in range(2)]
            act_c = sb("act_c", [P, FB, 512], where=l0)
            w3t = sb("w3t", [P, 4, P], where=l0)
        l1 = ExitStack()
        with l1:
            Ks = sb("Ks", [P, HG, TOK], F32R, where=l1)
            Qs = sb("Qs", [P, HG, TOK], F32R, where=l1)
            Qp = sb("Qp", [P, HG, G4, 512], F32R, where=l1)
            V = sb("V", [P, NT, H1 * VW], where=l1)
            hi = sb("hi", [P, 2, 512], F32R, where=l1)
            probs = sb("probs", [P, 8, 512], where=l1)
            mx = sb("mx", [P, 2, 16, 2], where=l1)
            mn = sb("mn", [P, 16], where=l1)
            m2 = sb("m2", [P, 4, 8], where=l1)
            mhi = sb("mhi", [P, 16], F32R, where=l1)
            mT = sb("mT", [8, 512], F32R, where=l1)
            U = sb("U", [P, 512], where=l1)
            rden = sb("rden", [P, 4, G4], where=l1)
        l2 = ExitStack()
        with l2:
            hT1 = [sb(f"hT1_{i}", [P, TOK], F32R, where=l2) for i in range(2)]
            rw1_ = [sb(f"rw1_{i}", [P, FF], F32R, where=l2) for i in range(2)]
            ew1_ = [sb(f"ew1_{i}", [P, EXP * FF], F32R, where=l2) for i in range(2)]
            OnT = sb("OnT", [P, 2, 512], where=l2)
            yT = sb("yT", [P, 2, 512], where=l2)
            rh = sb("rh", [P, FB, 512], where=l2)
            eh = sb("eh", [P, 2, FB, 512], where=l2)
            scT = sb("scT", [8, 512], where=l2)
            sc = sb("sc", [P, 4, 8], where=l2)
            cmp = sb("cmp", [P, 4, 8, 8], where=l2)
            tie = sb("tie", [P, 4, 8, 8], where=l2)
            rank = sb("rank", [P, 4, 8], where=l2)
            top = sb("top", [P, 4], where=l2)
            gs = sb("gs", [P, 4], where=l2)
            gate = sb("gate", [P, 4, 8], where=l2)
            gtT = sb("gtT", [8, 512], where=l2)
            acc = sb("acc", [P, 4, P], where=l2)

        def columns(tensor, pack):
            at, views = 0, {}
            for name, n in pack:
                views[name] = tensor[:, at:at + n]
                at += n
            return views

        cw, dw_, sw, fw, aw, mw = (columns(t, p) for t, p in ((CW, CONSTS), (DW, MODS), (SW, SPECTRAL), (FW, FFN),
                                                              (AW, ATTN), (MW, MOE)))
        ident = cw["ident"]

        def wide(ap, shape, axis):
            return ap.unsqueeze(axis).broadcast_to(shape)

        def bank(n):
            return ps[:, n, :]

        def tiles4(ap):
            return ap.rearrange("p (t d) -> p t d", t=4)

        def cols(i, size):
            return slice(i * size, (i + 1) * size) if isinstance(i, int) else bass.ts(i, size)

        def due(count):
            return not isinstance(count, int) or count > 0

        def spectrum(b):
            return ps[:, b, 0:4 * 2 * M].rearrange("p (c r f) -> p r c f", r=2, f=M)

        turn_kt, rows_kt = 2, 13
        score_bank, order = [], [4, 5, 7]
        for n in range(64):
            lent = any(4 * kt + 3 <= n <= 4 * kt + 6 for kt in (turn_kt, rows_kt))
            b = next(b for b in order if not (lent and b == 7))
            order = [o for o in order if o != b] + [b]
            score_bank.append(b)

        def items_since(n):
            return next(d for d in range(1, 64) if score_bank[(n - d) % 64] == score_bank[n])

        def last_in_bank_7(kt):
            return max(n for n in range(4 * kt + 4) if score_bank[n] == 7)

        stacks = [(0, 0, tb) for tb in range(TB)] + [(1, 0, 0)] + [(0, 1, tb) for tb in range(TB)] \
            + [(1, hg, 0) for hg in range(1, HG)] + [(0, hg, tb) for hg in range(2, HG) for tb in range(TB)] \
            + [(1, hg, tb) for hg in range(HG) for tb in range(1, TB)]
        early = 5

        def between(slot):
            total = len(stacks) - early + NT // 2
            lo, hi_ = early + total * slot // 32, early + total * (slot + 1) // 32
            n = len(stacks)
            return range(min(lo, n), min(hi_, n)), range(max(lo, n) - n, max(hi_, n) - n)

        groups = [(ri, j) for ri in range(2) for j in range(KV)]
        low_bank = (0, 1, 4, 5)

        mod_cols = modv[:, :].rearrange("p (k three) -> p k three", three=3)
        shift, gate_raw = mod_cols[:, :, 0], mod_cols[:, :, 2]

        block_ = ctx.enter_context(nc.Block())

        @block_.sync
        def _(sp):
            x_tiles = x_in.rearrange("(t p) d -> p t d", p=P)
            for b in range(TB):
                sp.dma_start(x[:, 4 * b:4 * b + 4, :], x_tiles[:, 4 * b:4 * b + 4, :]).then_inc(sem.x_in, 16)
            sp.dma_start(CW[:, :], consts_in).then_inc(sem.consts_in, 16)
            sp.dma_start(FW[:, :], ffn_in).then_inc(sem.ffn_in, 16)
            sp.dma_start(AW[:, :], attn_in).then_inc(sem.attn_in, 16)
            sp.dma_start(MW[:, :], moe_in).then_inc(sem.moe_in, 16)
            def put_max(qb, hg):
                sp.wait_ge(sem.mT_copied, 4 * qb + hg + 1)
                for part in range(2):
                    for g in range(G4):
                        row = 32 * g + 24 + part
                        sp.dma_start(Qp[row:row + 1, hg, g, :].bitcast(F32),
                                     mT[4 * part + g:4 * part + g + 1, :].bitcast(F32)) \
                          .then_inc(sem.mrow_in, 16)
            with sp.Fori(0, TB) as qb:
                for hg in range(HG):
                    put_max(qb, hg)
            out_tiles = out.rearrange("(t p) d -> p t d", p=P)
            for b in range(TB):
                sp.wait_ge(sem.x3_ready, b + 1)
                sp.dma_start(out_tiles[:, 4 * b:4 * b + 4, :], x[:, 4 * b:4 * b + 4, :]).then_inc(sem.out_done, 16)
            sp.wait_ge(sem.out_done, 16 * TB)

        @block_.gpsimd
        def _(pool):
            pool.memset(xhi[:, :, :, 0:KS - 1], 0.0).then_inc(sem.pad_zero, 1)
            pool.memset(Kp[:, :, :, :], 0.0).then_inc(sem.kv_zero, 1)
            pool.wait_ge(sem.mods_in, 16)
            pool.tensor_copy(mrow[:, :], dw_["mask_row"][0:32, :]).then_inc(sem.mask_ready, 1)
            pool.tensor_copy(mcol[:, :], dw_["mask_col"][0:32, :]).then_inc(sem.mask_ready, 1)
            pool.wait_ge(sem.x1_ready, TB)
            pool.wait_ge(sem.ffn_in, 16)
            pool.tensor_copy(h2_[0][:, :], fw["h2"]).then_inc(sem.w2_split, 1)
            pool.wait_ge(sem.w2_split, 1)
            pool.tensor_tensor(h2_[1][:, :], fw["h2"], h2_[0][:, :].bitcast(F32), ALU.subtract) \
                .then_inc(sem.w2_split, 1)
            pool.wait_ge(sem.x2_ready, TB)
            pool.memset(Qp[:, :, :, :].bitcast(F32), 0.0).then_inc(sem.qpad_zero, 1)
            pool.wait_ge(sem.qpad_zero, 1)

            def fill(qb, hg):
                if not (isinstance(qb, int) and qb == 0):
                    pool.wait_ge(sem.st_ready, 64 * (4 * (qb - 1) + hg + 1))
                for g in range(G4):
                    rows = slice(32 * g, 32 * g + 32)
                    pool.tensor_copy(Qp[rows, hg, g, :], Qs[rows, hg, cols(qb, 512)]) \
                        .then_inc(sem.qpad_filled, 1)

            for hg in range(1, HG):
                pool.wait_ge(sem.kq_done, stacks.index((1, hg, 0)) + 1)
                fill(0, hg)
            pool.wait_ge(sem.kq_done, len(stacks))
            with pool.Fori(1, TB) as qb:
                for hg in range(HG):
                    fill(qb, hg)

        @block_.scalar
        def _(act):
            act.dma_start(DW[:, :], mods_in).then_inc(sem.mods_in, 16)
            act.dma_start(SW[:, :], spectral_in).then_inc(sem.spectral_in, 16)
            act.wait_ge(sem.mods_in, 16)
            act.activation(silu[:, :], dw_["c"], ACT.Sigmoid).then_inc(sem.silu_sig, 1)
            act.wait_ge(sem.spectral_in, 16)
            act.activation(al[:, :], sw["alpha"], ACT.Sigmoid).then_inc(sem.alpha_ready, 1)

            def ln_std(k):
                act.wait_ge(sem.ln_var, k + 1)
                act.activation(sd[:, :], ve[:, :], ACT.Sqrt).then_inc(sem.ln_std, 1)

            def ln_out(k):
                for b in range(TB):
                    act.wait_ge(sem.zT_ready, TB * (k - 1) + b + 1)
                    act.activation(hT[:, 512 * b:512 * b + 512], bank(1 + b), ACT.Identity,
                                   bias=modv[:, 3 * k:3 * k + 1], scale=cv[:, k:k + 1]).then_inc(sem.hT_ready, 1)
                    if k != 2:
                        first = (hT0 if k == 1 else hT1)[0]
                        act.activation(first[:, 512 * b:512 * b + 512], bank(1 + b), ACT.Identity,
                                       bias=modv[:, 3 * k:3 * k + 1], scale=cv[:, k:k + 1]) \
                           .then_inc(sem.hT_first, 1)

            ln_std(0)
            act.wait_ge(sem.vec, 11)
            act.wait_ge(sem.pad_zero, 1)
            for u in range(8):
                act.wait_ge(sem.dft_ready, u + 1)
                sp_ = spectrum(u % 4)
                act.activation(xhi[:, :, 4 * u:4 * u + 4, KS - 1:], sp_[:, :, :, KL:M], ACT.Identity,
                               scale=cv[:, 0:1]).then_inc(sem.spec_copied, 1)
                act.activation(xlo[:, :, 4 * u:4 * u + 4, :], sp_[:, :, :, 0:KL], ACT.Identity,
                               scale=cv[:, 0:1]).then_inc(sem.spec_copied, 1)
            for n in range(4):
                act.wait_ge(sem.qkv_ready, n + 1)
                act.activation(QT[:, 2 * n:2 * n + 2, :], bank(4 + n).rearrange("p (b n) -> p b n", b=2),
                               ACT.Copy).then_inc(sem.q_copied, 1)
            act.wait_ge(sem.qkv_ready, 5)
            act.wait_ge(sem.kv_zero, 1)
            for half in range(2):
                rows = slice(64 * half, 64 * half + 64)
                act.activation(Kp[rows, :, half::2, :],
                               ps[rows, 0, :].rearrange("p (j r n) -> p r j n", j=2, r=2), ACT.Copy) \
                   .then_inc(sem.kv_copied, 1)
            act.wait_ge(sem.qkv_ready, 6)
            act.activation(Vl[:, :, :], bank(1).rearrange("p (r n) -> p r n", r=2), ACT.Copy) \
               .then_inc(sem.kv_copied, 1)
            act.wait_ge(sem.qkv_ready, 7)
            act.activation(g_sb[:, :], ps[:, 2, 0:NCH], ACT.Sigmoid, scale=1.0 / C).then_inc(sem.g_ready, 1)
            def low_exp(i):
                act.wait_ge(sem.s_sub, i + 1)
                act.activation(Pn[:, i % 2, :, :], Pn[:, i % 2, :, :], ACT.Exp, scale=float(HD) ** -0.5) \
                   .then_inc(sem.s_exp, 1)

            low_exp(0)
            for i, (ri, j) in enumerate(groups):
                if i + 1 < len(groups):
                    low_exp(i + 1)
                act.wait_ge(sem.pT_ready, i + 1)
                act.activation(PT[:, i % 2, :], bank(2 + i % 2), ACT.Copy).then_inc(sem.pT_copied, 1)
                act.wait_ge(sem.o_ready, i + 1)
                rows = slice(64 * (j % 2), 64 * (j % 2) + 64)
                act.activation(OT[rows, 4 * (j // 2):4 * (j // 2) + 4, ri, :],
                               ps[rows, 2 + i % 2, :].rearrange("p (b n) -> p b n", b=4), ACT.Copy) \
                   .then_inc(sem.o_copied, 1)
            for ri in range(2):
                act.wait_ge(sem.conv_step, 2 * KS - 1 + ri)
                act.activation(cacc[:, ri, :, :], cacc[:, ri, :, :], ACT.Gelu).then_inc(sem.gelu_ready, 1)
            for b in range(4):
                act.wait_ge(sem.yT_ready, b + 1)
                act.activation(YT[:, 4 * b:4 * b + 4, :], tiles4(bank(1 + b)), ACT.Copy).then_inc(sem.yT_copied, 1)
            for n in range(2):
                act.wait_ge(sem.bcast_ready, 2)
                act.activation(gb[:, n, :], ps[:, 7, n * P:n * P + P], ACT.Copy).then_inc(sem.bcast_copied, 1)
            ln_std(1)
            act.wait_ge(sem.ffn_in, 16)
            act.wait_ge(sem.x1_ready, TB)
            act.activation(w1_[0][:, 0, :], fw["w1"], ACT.Copy).then_inc(sem.w_first, 1)
            act.activation(w1_[0][:, 1, :], fw["w2"], ACT.Copy).then_inc(sem.w_first, 1)
            act.activation(h1_[0][:, :], fw["h1"], ACT.Copy).then_inc(sem.w_first, 1)
            ln_out(1)

            act.wait_ge(sem.vec, 19)

            def ffn_gates(tb):
                def first_part(fb):
                    act.wait_ge(sem.af_ready, 4 * tb + fb + 1)
                    act.activation(act_a[0][:, fb, :], af[:, fb % 2, :], ACT.Copy).then_inc(sem.ah_ready, 1)

                for fb in range(FB):
                    act.wait_ge(sem.u_ready, 4 * tb + fb + 1)
                    act.activation(tanh_t[:, fb % 2, :], bank(fb % 2), ACT.Tanh, scale=hs[:, fb:fb + 1]) \
                       .then_inc(sem.t_ready, 1)
                    if fb:
                        first_part(fb - 1)
                first_part(FB - 1)

            def ffn_b(tb):
                for ob in range(FB):
                    act.wait_ge(sem.h_ready, 8 * tb + ob + 1)
                    act.activation(act_b[0][:, ob, :], bank(4 + ob % 2), ACT.Gelu, scale=fw["hs1"][:, ob:ob + 1]) \
                       .then_inc(sem.bh_ready, 1)
                    if due(4 * tb + ob - 1):
                        act.wait_ge(sem.b_ready, 4 * tb + ob - 1)
                    act.activation(bf[:, ob % 2, :], bank(4 + ob % 2), ACT.Gelu, scale=fw["hs1"][:, ob:ob + 1]) \
                       .then_inc(sem.hb_free, 1)

            def ffn_c(tb):
                for ob in range(FB):
                    act.wait_ge(sem.h_ready, 8 * tb + 4 + ob + 1)
                    act.activation(act_c[:, ob, :], bank(4 + ob % 2), ACT.Gelu, scale=fw["hs2"][:, ob:ob + 1]) \
                       .then_inc(sem.hb_free, 1)

            ffn_gates(0)
            ffn_b(0)
            ffn_gates(1)
            ffn_c(0)
            with act.Fori(1, TB - 1) as tb:
                ffn_b(tb)
                ffn_gates(tb + 1)
                ffn_c(tb)
            ffn_b(TB - 1)
            ffn_c(TB - 1)

            ln_std(2)
            ln_out(2)
            act.wait_ge(sem.attn_in, 16)
            for n, (kq, hg, tb) in enumerate(stacks):
                act.wait_ge(sem.kq_ready, n + 1)
                if due(n - 1):
                    act.wait_ge(sem.kq_done, n - 1)
                act.activation(hi[:, n % 2, :], bank(4 + n % 4), ACT.Identity, bias=(kb_lo, qb_lo)[kq][:, hg:hg + 1],
                               scale=cw[("lo_k", "lo_q")[kq]]).then_inc(sem.kq_hi, 1)
                if n == early - 1:
                    act.wait_ge(sem.qpad_zero, 1)
                    act.wait_ge(sem.kq_done, early)
                    for g in range(G4):
                        rows = slice(32 * g, 32 * g + 32)
                        act.activation(Qp[rows, 0, g, :], Qs[rows, 0, 0:512].bitcast(F32), ACT.Copy) \
                           .then_inc(sem.first_filled, 1)

            def exps(qb, s):
                for g in range(G4):
                    if s % 16 == 0 and g == 2 and not (isinstance(qb, int) and qb == 0 and s < 16):
                        grp = 4 * qb + s // 16
                        act.wait_ge(sem.pv_ready, 16 * grp)
                        act.wait_ge(sem.o_norm, grp)
                        act.activation(U[:, :], bank(6), ACT.Copy).then_inc(sem.u_copied, 1)
                    n = 256 * qb + 4 * s + g
                    if g == 0:
                        if due(64 * qb + s - 1):
                            act.wait_ge(sem.pv_ready, 64 * qb + s - 1)
                    act.wait_ge(sem.st_ready, n + 1)
                    act.activation(probs[:, 4 * (s % 2) + g, :], bank(score_bank[4 * (s % 16) + g]), ACT.Exp, scale=SCALE1) \
                       .then_inc(sem.exp_done, 1)

            for s in range(4):
                exps(0, s)
            with act.Fori(0, TB - 1) as qb:
                for s in range(4, 68):
                    exps(qb, s)
            for s in range(4, 64):
                exps(TB - 1, s)
            act.wait_ge(sem.pv_ready, 256)
            act.wait_ge(sem.o_norm, 16)
            act.activation(U[:, :], bank(6), ACT.Copy).then_inc(sem.u_copied, 1)

            def fc_in(b):
                act.wait_ge(sem.oT_ready, b + 1)
                act.activation(OnT[:, b % 2, :], bank(b % 2), ACT.Copy).then_inc(sem.oT_copied, 1)

            act.wait_ge(sem.moe_in, 16)
            act.activation(rw1_[0][:, :], mw["rw1"], ACT.Copy).then_inc(sem.e_first, 1)

            def split_experts(e):
                act.activation(ew1_[0][:, e * FF:e * FF + FF], mw["ew1"][:, e * FF:e * FF + FF], ACT.Copy) \
                   .then_inc(sem.e_first, 1)

            fc_in(0)
            for b in range(TB):
                if b + 1 < TB:
                    fc_in(b + 1)
                for e in range(2 * b, 2 * b + 2):
                    split_experts(e)
                act.wait_ge(sem.fc_ready, b + 1)
                if due(b - 1):
                    act.wait_ge(sem.yn_ready, b - 1)
                act.activation(yT[:, b % 2, :], bank(2 + b % 2), ACT.Identity, bias=fcbg[:, 0:1],
                               scale=gv[:, 2:3]).then_inc(sem.fc_copied, 1)
            ln_std(3)
            ln_out(3)

            def moe(tb):
                for fb in range(FB):
                    act.wait_ge(sem.rh_ready, 4 * tb + fb + 1)
                    act.activation(rh[:, fb, :], bank(4 + fb % 2), ACT.Relu, bias=mw["rb1"][:, fb:fb + 1]) \
                       .then_inc(sem.rh_copied, 1)

                def hidden(e):
                    for fb in range(FB):
                        act.wait_ge(sem.eh_ready, 32 * tb + 4 * e + fb + 1)
                        col = e * FB + fb
                        act.activation(eh[:, e % 2, fb, :], bank(fb % 2), ACT.Relu,
                                       bias=mw["eb1"][:, col:col + 1]).then_inc(sem.eh_copied, 1)

                act.wait_ge(sem.sc_ready, tb + 1)
                act.activation(scT[:, :], ps[0:8, 6, :], ACT.Copy).then_inc(sem.sc_copied, 1)
                hidden(0)
                hidden(1)
                act.wait_ge(sem.gt_step, 13 * tb + 8)
                act.activation(gate[:, :, :], sc[:, :, :], ACT.Exp).then_inc(sem.gate_ready, 1)
                act.wait_ge(sem.gtT_ready, tb + 1)
                act.activation(gtT[:, :], ps[0:8, 6, :], ACT.Copy).then_inc(sem.gtT_copied, 1)
                for e in range(2, EXP):
                    hidden(e)

            moe(0)
            with act.Fori(1, TB) as tb:
                moe(tb)

        @block_.tensor
        def _(pe):
            pe.wait_ge(sem.mods_in, 16)
            pe.wait_ge(sem.silu_ready, 1)
            for layer in range(2):
                for k in range(6):
                    last = pe.matmul(ps[:, 7, 6 * layer + k:6 * layer + k + 1],
                                     dw_[f"wmod{layer}"][:, k * P:k * P + P], silu[:, layer:layer + 1],
                                     start=True, stop=True)
            last.then_inc(sem.mod_ready, 1)
            for u in range(8):
                pe.wait_ge(sem.ln_z, 1 + 2 * (u + 1))
                if u >= 4:
                    pe.wait_ge(sem.spec_copied, 2 * (u - 3))
                for i in range(2):
                    last = pe.matmul(ps[:, u % 4, i * 4 * M:(i + 1) * 4 * M], z[:, 2 * u + i, :], dw_["dft"],
                                     start=True, stop=True)
                last.then_inc(sem.dft_ready, 1)
            low_flat = xlo[:, :, :, :].rearrange("p r c k -> p (r c k)")
            pe.wait_ge(sem.spec_copied, 16)
            pe.wait_ge(sem.dc_ready, 1)
            pe.wait_ge(sem.spectral_in, 16)
            pe.wait_ge(sem.vec, 1)
            for n in range(4):
                for i in range(2):
                    b = 2 * n + i
                    last = pe.matmul(ps[:, 4 + n, 256 * i:256 * i + 256], sw["qw"][:, b * P:b * P + P], low_flat,
                                     start=True, stop=True)
                last.then_inc(sem.qkv_ready, 1)
            for j in range(2):
                last = pe.matmul(ps[:, 0, 256 * j:256 * j + 256], sw["kw"][:, j * P:j * P + P], low_flat,
                                 start=True, stop=True)
            last.then_inc(sem.qkv_ready, 1)
            for ri in range(2):
                last = pe.matmul(ps[:, 1, 256 * ri:256 * ri + 256], low_flat[:, ri * P:ri * P + P], sw["vw"],
                                 start=True, stop=True)
            last.then_inc(sem.qkv_ready, 1)
            pe.matmul(ps[:, 2, 0:NCH], sw["gate_w"], xlo[:, 0, :, 0], start=True, stop=True) \
              .then_inc(sem.qkv_ready, 1)
            pe.wait_ge(sem.kv_copied, 3)
            pe.wait_ge(sem.g_ready, 1)
            pe.wait_ge(sem.mask_ready, 2)
            pe.wait_ge(sem.consts_in, 16)

            def low_scores(i):
                ri, j = groups[i]
                if due(i - 3):
                    pe.wait_ge(sem.s_sub, i - 3)
                pe.matmul(bank(low_bank[i % 4]), mrow[:, :], mcol[:, :], start=True, stop=False, skip_group_check=True)
                for b in range(G4):
                    last = pe.matmul(ps[:, low_bank[i % 4], b * P:b * P + P],
                                     QT[:, 4 * (j // 2) + b, ri * P:ri * P + P], Kp[:, ri, j, :],
                                     start=False, stop=(b == G4 - 1), skip_group_check=True)
                last.then_inc(sem.s_ready, 1)

            pe.wait_ge(sem.q_copied, 4)
            for i in range(4):
                low_scores(i)
            for i, (ri, j) in enumerate(groups):
                pe.wait_ge(sem.p_ready, i + 1)
                if due(i - 1):
                    pe.wait_ge(sem.o_copied, i - 1)
                for b in range(G4):
                    last = pe.transpose(ps[:, 2 + i % 2, b * P:b * P + P], Pn[:, i % 2, b, :], ident)
                last.then_inc(sem.pT_ready, 1)
                if i + 4 < len(groups):
                    low_scores(i + 4)
                pe.wait_ge(sem.pT_copied, i + 1)
                row = 64 * (j % 2)
                pe.matmul(ps[row:row + 64, 2 + i % 2, :], Vl[:, ri, 64 * j:64 * j + 64], PT[:, i % 2, :],
                          start=True, stop=True).then_inc(sem.o_ready, 1)
            pe.wait_ge(sem.o_copied, 8)
            for b in range(8):
                last = pe.matmul(ps[:, 0, 0:256], sw["ow"][:, b * P:b * P + P],
                                 OT[:, b, :, :].rearrange("p r n -> p (r n)"), start=(b == 0), stop=(b == 7))
            last.then_inc(sem.aT_ready, 1)
            for ri in range(2):
                pe.wait_ge(sem.gelu_ready, ri + 1)
                for half in range(2):
                    n = 2 * ri + half
                    pe.matmul(ps[:, 4 + n, 0:16 * NH_], sw[("pw_r", "pw_i")[ri]],
                              cacc[:, ri, 16 * half:16 * half + 16, :].rearrange("p c f -> p (c f)"),
                              start=True, stop=True).then_inc(sem.pw_ready, 1)
            pe.wait_ge(sem.y_ready, 6)
            for b in range(4):
                for i in range(4):
                    t = 4 * b + i
                    last = pe.transpose(ps[:, 1 + b, i * P:i * P + P],
                                        Y[:, 2 * t:2 * t + 2, :].rearrange("p c k -> p (c k)"), ident)
                last.then_inc(sem.yT_ready, 1)
            for b in range(4):
                pe.wait_ge(sem.yT_copied, b + 1)
                pe.matmul(bank((5 + b) % 8), dw_["idft"], YT[:, 4 * b:4 * b + 4, :].rearrange("p t d -> p (t d)"),
                          start=True, stop=True).then_inc(sem.idft_ready, 1)
            pe.wait_ge(sem.diag_ready, 1)
            pe.wait_ge(sem.x1_ready, TB)
            for n in range(2):
                pe.matmul(ps[:, 7, n * P:n * P + P], cw["ones"], diag[:, n, :], start=True, stop=True) \
                  .then_inc(sem.bcast_ready, 1)

            def z_transposes(k):
                for b in range(TB):
                    pe.wait_ge(sem.ln_z, 17 * k + 1 + 4 * (b + 1))
                    for i in range(4):
                        last = pe.transpose(ps[:, 1 + b, i * P:i * P + P], z[:, 4 * b + i, :], ident)
                    last.then_inc(sem.zT_ready, 1)
                pe.wait_ge(sem.hT_ready, TB * k)

            z_transposes(1)
            pe.wait_ge(sem.ffn_in, 16)
            pe.wait_ge(sem.bcast_copied, 2)

            def three(to, w, v, start, stop):
                pe.matmul(to, w[0], v[0], start=start, stop=False)
                pe.matmul(to, w[0], v[1], start=False, stop=False)
                return pe.matmul(to, w[1], v[0], start=False, stop=stop)

            def both(parts, *where):
                return [p[where] for p in parts]

            every = slice(None)

            def ffn_up(tb):
                v = both(hT0, every, cols(tb, 512))
                for fb in range(FB):
                    if due(4 * tb + fb - 1):
                        pe.wait_ge(sem.af_ready, 4 * tb + fb - 1)
                    three(bank(fb % 2), both(w1_, every, 0, slice(fb * P, fb * P + P)), v, True, True)
                    three(bank(2 + fb % 2), both(w1_, every, 1, slice(fb * P, fb * P + P)), v, True, True) \
                        .then_inc(sem.u_ready, 1)

            def ffn_hidden(tb, half):
                src, w, ready = ((act_a, h1_, sem.a_ready), (act_b, h2_, sem.b_ready))[half]
                for ob in range(FB):
                    if due(8 * tb + 4 * half + ob - 1):
                        pe.wait_ge(sem.hb_free, 8 * tb + 4 * half + ob - 1)
                    for fb in range(FB):
                        if ob == 0:
                            pe.wait_ge(ready, 4 * tb + fb + 1)
                        col = fb * FF + ob * P
                        last = three(bank(4 + ob % 2), both(w, every, slice(col, col + P)),
                                     both(src, every, fb), fb == 0, fb == FB - 1)
                    last.then_inc(sem.h_ready, 1)

            def ffn_down(tb):
                pe.wait_ge(sem.hb_free, 8 * tb + 8)
                if due(tb):
                    pe.wait_ge(sem.w3_scaled, tb)
                for qt in range(4):
                    for fb in range(FB):
                        last = pe.matmul(ps[:, 6, qt * P:qt * P + P], act_c[:, fb, qt * P:qt * P + P],
                                         fw["w3"][:, fb * P:fb * P + P], start=(fb == 0), stop=(fb == FB - 1))
                last.then_inc(sem.w3_ready, 1)

            pe.wait_ge(sem.hT_second, TB)
            pe.wait_ge(sem.w_second, 2)
            ffn_up(0)
            pe.wait_ge(sem.w_second, 3)
            ffn_hidden(0, 0)
            ffn_up(1)
            pe.wait_ge(sem.w2_split, 2)
            ffn_hidden(0, 1)
            with pe.Fori(1, TB - 1) as tb:
                ffn_hidden(tb, 0)
                ffn_down(tb - 1)
                ffn_up(tb + 1)
                ffn_hidden(tb, 1)
            ffn_hidden(TB - 1, 0)
            ffn_down(TB - 2)
            ffn_hidden(TB - 1, 1)
            ffn_down(TB - 1)

            z_transposes(2)
            pe.wait_ge(sem.attn_in, 16)
            def stack(n):
                kq, hg, tb = stacks[n]
                if due(n - 3):
                    pe.wait_ge(sem.kq_done, n - 3)
                pe.matmul(bank(4 + n % 4), aw[("kw1", "qw1")[kq]][:, hg * P:hg * P + P],
                          hT[:, tb * 512:tb * 512 + 512], start=True, stop=True).then_inc(sem.kq_ready, 1)

            def value_tiles(u):
                pe.wait_ge(sem.kq_done, min(len(stacks), len(stacks) - 3 + u))
                if due(u - 3):
                    pe.wait_ge(sem.v_copied, u - 3)
                for i in range(2):
                    t = 2 * u + i
                    last = pe.matmul(ps[:, 4 + u % 4, 256 * i:256 * i + 256], hT[:, t * P:t * P + P], aw["vw1"],
                                     start=True, stop=True)
                last.then_inc(sem.v_ready, 1)

            def nat(qb, k, c):
                hg, qt, g = k // 16 % 4, k % 16 // 4, k % 4
                item = 64 * qb + k
                if c == 0 and k % 16 == 0:
                    if isinstance(qb, int) and qb == 0 and k == 0:
                        pe.wait_ge(sem.first_filled, G4)
                    else:
                        pe.wait_ge(sem.qpad_filled, 4 * (4 * qb + k // 16))
                if c % 2 == 0:
                    if due(2 * item + c // 2 - 1):
                        pe.wait_ge(sem.nat_max, 2 * item + c // 2 - 1)
                mm = pe.matmul(bank(c), Qp[:, hg, g, qt * P:qt * P + P], Ks[:, hg, c * 512:c * 512 + 512],
                               start=True, stop=True)
                if c % 2:
                    mm.then_inc(sem.nat_ready, 1)

            def max_rows(qb, grp):
                pe.wait_ge(sem.m_step, 4 * (4 * qb + grp + 1))
                if due(4 * qb + grp):
                    pe.wait_ge(sem.o_norm, 4 * qb + grp)
                    pe.wait_ge(sem.exp_done, 256 * qb + 64 * (grp - 1) + last_in_bank_7(rows_kt) + 1)
                for qt in range(4):
                    last = pe.transpose(ps[0:8, 7, qt * P:qt * P + P], m2[:, qt, :], ident)
                last.then_inc(sem.mT_ready, 1)

            def turn_outputs(qb, grp):
                pe.wait_ge(sem.u_copied, 4 * qb + grp)
                pe.wait_ge(sem.o_norm, 4 * qb + grp)
                pe.wait_ge(sem.mT_copied, 4 * qb + grp + 1 if not (isinstance(qb, int) and 4 * qb + grp == 16) else 16)
                if isinstance(qb, int) and 4 * qb + grp == 16:
                    pe.wait_ge(sem.exp_done, 1024)
                else:
                    pe.wait_ge(sem.exp_done, 256 * qb + 64 * grp + last_in_bank_7(turn_kt) + 1)
                for qt in range(4):
                    last = pe.transpose(ps[:, 7, qt * P:qt * P + P], U[:, qt * P:qt * P + P], ident)
                last.then_inc(sem.uT_ready, 1)

            def values(qb, s):
                hg, kt = s // 16 % 4, s % 16
                if kt == 0:
                    if due(4 * qb + s // 16):
                        pe.wait_ge(sem.u_copied, 4 * qb + s // 16)
                for g in range(G4):
                    pe.wait_ge(sem.exp_done, 256 * qb + 4 * s + g + 1)
                    col = (4 * hg + g) * VW
                    last = pe.matmul(ps[32 * g:32 * g + VW, 6, :], V[:, kt, col:col + VW],
                                     probs[:, 4 * (s % 2) + g, :], start=(kt == 0), stop=(kt == 15))
                last.then_inc(sem.pv_ready, 1)

            def step(qb, s):
                hg, kt = s // 16 % 4, s % 16
                last_block = isinstance(qb, int) and qb == TB - 1
                if kt == 0:
                    pe.wait_ge(sem.mrow_in, 128 * (4 * qb + s // 16 + 1))
                for g in range(G4):
                    if g == 2 and not (isinstance(qb, int) and qb == 0 and s == 0):
                        if not (last_block and s - 1 + LEAD >= 64):
                            nat(qb, s - 1 + LEAD, 3)
                        values(qb, s - 1)
                    n = 4 * kt + g
                    free = 256 * qb + 4 * s + g - items_since(n) + 1
                    if due(free):
                        pe.wait_ge(sem.exp_done, free)
                    if n > 4 * turn_kt + 6 and n == min(m for m in range(4 * turn_kt + 7, 64) if score_bank[m] == 7):
                        pe.wait_ge(sem.o_norm, 4 * qb + s // 16 + 1)
                    if n > 4 * rows_kt + 6 and n == min(m for m in range(4 * rows_kt + 7, 64) if score_bank[m] == 7) \
                            and not (last_block and s // 16 == 3):
                        pe.wait_ge(sem.mT_copied, 4 * qb + s // 16 + 2)
                    pe.matmul(bank(score_bank[n]), Ks[:, hg, kt * P:kt * P + P], Qp[:, hg, g, :],
                              start=True, stop=True).then_inc(sem.st_ready, 1)
                if not (last_block and s + LEAD >= 64):
                    for c in range(3):
                        nat(qb, s + LEAD, c)
                if kt == turn_kt and not (isinstance(qb, int) and qb == 0 and s < 16):
                    turn_outputs(qb, s // 16)
                if kt == rows_kt and not (last_block and s // 16 == 3):
                    max_rows(qb, s // 16 + 1)

            for n in range(early):
                stack(n)
            pe.wait_ge(sem.kq_done, early)
            for k in range(16):
                for half in range(2):
                    nat(0, k, 2 * half)
                    nat(0, k, 2 * half + 1)
                    some_stacks, some_values = between(2 * k + half)
                    for n in some_stacks:
                        stack(n)
                    for u in some_values:
                        value_tiles(u)
            pe.wait_ge(sem.v_copied, NT // 2)
            for k in range(16, LEAD):
                for c in range(4):
                    nat(0, k, c)
                if k == 16:
                    max_rows(0, 0)
            pe.wait_ge(sem.o_norm, 1)
            for s in range(4):
                step(0, s)
            with pe.Fori(0, TB - 1) as qb:
                for s in range(4, 68):
                    step(qb, s)
            for s in range(4, 64):
                step(TB - 1, s)
            values(TB - 1, 63)
            turn_outputs(TB - 1, 4)

            def turn_heads(b):
                pe.wait_ge(sem.o_norm, 17)
                for i in range(4):
                    last = pe.transpose(ps[:, b % 2, i * P:i * P + P], z[:, 4 * b + i, :], ident)
                last.then_inc(sem.oT_ready, 1)

            turn_heads(0)
            for b in range(TB):
                if b + 1 < TB:
                    if due(b):
                        pe.wait_ge(sem.oT_copied, b)
                    turn_heads(b + 1)
                pe.wait_ge(sem.oT_copied, b + 1)
                if due(b - 1):
                    pe.wait_ge(sem.fc_copied, b - 1)
                pe.matmul(bank(2 + b % 2), aw["fc"], OnT[:, b % 2, :], start=True, stop=False)
                pe.matmul(bank(2 + b % 2), ident, hT[:, 512 * b:512 * b + 512], start=False, stop=True) \
                  .then_inc(sem.fc_ready, 1)
                pe.wait_ge(sem.fc_copied, b + 1)
                if due(b - 1):
                    pe.wait_ge(sem.aux_ready, b - 1)
                for i in range(4):
                    last = pe.transpose(ps[:, 4 + b % 2, i * P:i * P + P], yT[:, b % 2, i * P:i * P + P], ident)
                last.then_inc(sem.yn_ready, 1)
            z_transposes(3)
            pe.wait_ge(sem.hT_first, 2 * TB)
            pe.wait_ge(sem.e_second, 1 + EXP)
            pe.wait_ge(sem.hT_second, 2 * TB)

            def moe(tb):
                v = both(hT1, every, cols(tb, 512))
                for fb in range(FB):
                    if due(4 * tb + fb - 1):
                        pe.wait_ge(sem.rh_copied, 4 * tb + fb - 1)
                    three(bank(4 + fb % 2), both(rw1_, every, slice(fb * P, fb * P + P)), v, True, True) \
                        .then_inc(sem.rh_ready, 1)
                if due(tb):
                    pe.wait_ge(sem.gtT_copied, tb)
                for fb in range(FB):
                    pe.wait_ge(sem.rh_copied, 4 * tb + fb + 1)
                    last = pe.matmul(ps[0:8, 6, :], mw["rw2"][:, fb * EXP:fb * EXP + EXP], rh[:, fb, :],
                                     start=(fb == 0), stop=(fb == FB - 1))
                last.then_inc(sem.sc_ready, 1)

                def up(e):
                    for fb in range(FB):
                        if due(32 * tb + 4 * e + fb - 1):
                            pe.wait_ge(sem.eh_copied, 32 * tb + 4 * e + fb - 1)
                        col = e * FF + fb * P
                        three(bank(fb % 2), both(ew1_, every, slice(col, col + P)), v, True, True) \
                            .then_inc(sem.eh_ready, 1)

                def down(e):
                    pe.wait_ge(sem.eh_copied, 32 * tb + 4 * e + 4)
                    if due(4 * (8 * tb + e - 1)):
                        pe.wait_ge(sem.acc_step, 4 * (8 * tb + e - 1))
                    for qt in range(4):
                        for fb in range(FB):
                            col = e * FF + fb * P
                            last = pe.matmul(ps[:, 2 + e % 2, qt * P:qt * P + P],
                                             eh[:, e % 2, fb, qt * P:qt * P + P], mw["ew2"][:, col:col + P],
                                             start=(fb == 0), stop=(fb == FB - 1))
                    last.then_inc(sem.ey_ready, 1)

                up(0)
                pe.wait_ge(sem.sc_copied, tb + 1)
                for qt in range(4):
                    last = pe.matmul(ps[:, 6, qt * 8:qt * 8 + 8], scT[:, qt * P:qt * P + P], ident[0:8, 0:8],
                                     start=True, stop=True)
                last.then_inc(sem.scT_ready, 1)
                up(1)
                down(0)
                pe.wait_ge(sem.gt_step, 13 * tb + 13)
                for qt in range(4):
                    last = pe.transpose(ps[0:8, 6, qt * P:qt * P + P], gate[:, qt, :], ident)
                last.then_inc(sem.gtT_ready, 1)
                up(2)
                pe.wait_ge(sem.gtT_copied, tb + 1)
                for qt in range(4):
                    last = pe.matmul(ps[:, 7, qt * P:qt * P + P], gtT[:, qt * P:qt * P + P], mw["eb2"][0:8, :],
                                     start=True, stop=True)
                last.then_inc(sem.b2_ready, 1)
                down(1)
                for e in range(3, EXP):
                    up(e)
                    down(e - 1)
                down(EXP - 1)

            moe(0)
            with pe.Fori(1, TB) as tb:
                moe(tb)

        @block_.vector
        def _(dve):
            def ln_stats(k, b):
                for t in range(4 * b, 4 * b + 4):
                    dve.bn_stats(st[:, t, :], x[:, t, :]).then_inc(sem.stats, 1)
                dve.wait_ge(sem.stats, 32 * k + 8 * b + 4)
                for t in range(4 * b, 4 * b + 4):
                    dve.bn_aggr(mv[:, t, :], st[:, t, :]).then_inc(sem.stats, 1)

            def ln(k):
                dve.wait_ge(sem.stats, 32 * k + 32)
                dve.tensor_scalar(ve[:, :], mv[:, :, 1], 1e-5, None, ALU.add).then_inc(sem.ln_var, 1)
                dve.wait_ge(sem.ln_std, k + 1)
                dve.reciprocal(rstd[:, :], sd[:, :]).then_inc(sem.ln_z, 1)
                dve.wait_ge(sem.ln_z, 17 * k + 1)
                for t in range(NT):
                    dve.tensor_scalar(z[:, t, :], x[:, t, :], mv[:, t, 0:1], rstd[:, t:t + 1],
                                      ALU.subtract, ALU.mult).then_inc(sem.ln_z, 1)

            dve.wait_ge(sem.mods_in, 16)
            dve.wait_ge(sem.silu_sig, 1)
            dve.tensor_tensor(silu[:, :], silu[:, :], dw_["c"], ALU.mult).then_inc(sem.silu_ready, 1)
            dve.wait_ge(sem.x_in, 64)
            for b in range(TB):
                ln_stats(0, b)
            ln(0)
            dve.wait_ge(sem.mod_ready, 1)
            dve.tensor_copy(modv[:, :], ps[:, 7, 0:12]).then_inc(sem.vec, 1)
            dve.wait_ge(sem.vec, 1)
            dve.tensor_scalar(cv[:, :], mod_cols[:, :, 1], 1.0, None, ALU.add).then_inc(sem.vec, 1)
            dve.wait_ge(sem.vec, 2)
            dve.tensor_scalar(gsgn[:, :], gate_raw, 0.0, 2.0, ALU.is_ge, ALU.mult).then_inc(sem.vec, 1)
            dve.wait_ge(sem.vec, 3)
            dve.tensor_scalar(gneg[:, :], gate_raw, -1.0, None, ALU.mult).then_inc(sem.vec, 1)
            dve.wait_ge(sem.vec, 4)
            dve.tensor_scalar(gsgn[:, :], gsgn[:, :], -1.0, None, ALU.add).then_inc(sem.vec, 1)
            dve.wait_ge(sem.vec, 5)
            dve.tensor_tensor(gabs[:, :], gate_raw, gneg[:, :], ALU.max).then_inc(sem.vec, 1)
            dve.wait_ge(sem.vec, 6)
            dve.tensor_scalar(gabs[:, :], gabs[:, :], 0.25, None, ALU.max).then_inc(sem.vec, 1)
            dve.wait_ge(sem.vec, 7)
            dve.tensor_tensor(gv[:, :], gsgn[:, :], gabs[:, :], ALU.mult).then_inc(sem.vec, 1)
            dve.wait_ge(sem.vec, 8)
            dve.tensor_scalar(dc[:, :], modv[:, 0:1], float(C), None, ALU.mult).then_inc(sem.vec, 1)
            dve.wait_ge(sem.vec, 9)
            dve.wait_ge(sem.alpha_ready, 1)
            dve.tensor_tensor(alg[:, :], al[:, :], gv[:, 0:1], ALU.mult).then_inc(sem.vec, 1)
            dve.wait_ge(sem.vec, 10)
            dve.tensor_tensor(alx[:, :], gv[:, 0:1], alg[:, :], ALU.subtract).then_inc(sem.vec, 1)
            dve.wait_ge(sem.vec, 11)
            dve.wait_ge(sem.spec_copied, 16)
            dve.tensor_scalar(xlo[:, 0, :, 0], xlo[:, 0, :, 0], dc[:, 0:1], None, ALU.add).then_inc(sem.dc_ready, 1)
            dve.wait_ge(sem.spectral_in, 16)
            def taps(steps):
                for j, ri in steps:
                    tap = sw[("dw_r", "dw_i")[ri]][:, j:j + 1]
                    src = xhi[:, ri, :, j:j + NH_]
                    if j == 0:
                        ins = dve.tensor_scalar(cacc[:, ri, :, :], src, tap, None, ALU.mult)
                    else:
                        dve.wait_ge(sem.conv_step, 2 * (j - 1) + ri + 1)
                        ins = dve.scalar_tensor_tensor(out=cacc[:, ri, :, :], in0=src, scalar=tap,
                                                       in1=cacc[:, ri, :, :], op0=ALU.mult, op1=ALU.add)
                    ins.then_inc(sem.conv_step, 1)

            conv = [(j, ri) for j in range(KS) for ri in range(2)]
            taps(conv[:10])

            def four(ap):
                return wide(ap, [P, G4, P], 2)

            def low_top(i):
                p = i % 2
                s4 = bank(low_bank[i % 4]).rearrange("p (b n) -> p b n", b=G4)
                dve.wait_ge(sem.s_ready, i + 1)
                if due(i - 1):
                    dve.wait_ge(sem.pT_ready, i - 1)
                dve.tensor_reduce(smax[:, p, :], s4, AX, ALU.max).then_inc(sem.s_max, 1)
                dve.wait_ge(sem.s_max, i + 1)
                dve.tensor_tensor(Pn[:, p, :, :], s4, four(smax[:, p, :]), ALU.subtract).then_inc(sem.s_sub, 1)

            low_top(0)
            for i in range(len(groups)):
                p = i % 2
                if i + 1 < len(groups):
                    low_top(i + 1)
                taps(conv[10 + i:11 + i])
                dve.wait_ge(sem.s_exp, i + 1)
                dve.tensor_reduce(ssum[:, p, :], Pn[:, p, :, :], AX, ALU.add).then_inc(sem.s_sum, 1)
                dve.wait_ge(sem.s_sum, i + 1)
                dve.reciprocal(srcp[:, p, :], ssum[:, p, :]).then_inc(sem.s_rcp, 1)
                dve.wait_ge(sem.s_rcp, i + 1)
                dve.tensor_tensor(Pn[:, p, :, :], Pn[:, p, :, :], four(srcp[:, p, :]), ALU.mult) \
                   .then_inc(sem.p_ready, 1)

            dve.tensor_scalar(lowt[:, :, :, :], xlo[:, :, :, :], alx[:, 0:1], None, ALU.mult).then_inc(sem.low_step, 1)
            dve.wait_ge(sem.low_step, 1)
            dve.wait_ge(sem.aT_ready, 1)
            aT = ps[:, 0, 0:256].rearrange("p (r c k) -> p r c k", r=2, k=KL)
            for ri in range(2):
                dve.scalar_tensor_tensor(out=Y[:, :, M * ri:M * ri + KL - ri], in0=aT[:, ri, :, ri:KL],
                                         scalar=alg[:, 0:1], in1=lowt[:, ri, :, ri:KL], op0=ALU.mult, op1=ALU.add) \
                   .then_inc(sem.y_ready, 1)
            dve.wait_ge(sem.g_ready, 1)
            for n in range(4):
                ri, c = n // 2, slice(16 * (n % 2), 16 * (n % 2) + 16)
                dve.wait_ge(sem.pw_ready, n + 1)
                tmp = cacc[:, ri, c, :]
                dve.scalar_tensor_tensor(
                    out=tmp, in0=ps[:, 4 + n, 0:16 * NH_].rearrange("p (c f) -> p c f", f=NH_), scalar=gv[:, 0:1],
                    in1=wide(g_sb[:, c], [P, 16, NH_], 2), op0=ALU.mult, op1=ALU.mult).then_inc(sem.pw_step, 1)
                dve.wait_ge(sem.pw_step, n + 1)
                keep = NH_ - ri
                to = M + KL - 1 if ri else KL
                dve.scalar_tensor_tensor(out=Y[:, c, to:to + keep], in0=xhi[:, ri, c, KS - 1:KS - 1 + keep],
                                         scalar=gv[:, 0:1], in1=tmp[:, :, 0:keep], op0=ALU.mult, op1=ALU.add) \
                   .then_inc(sem.y_ready, 1)
            dve.wait_ge(sem.ffn_in, 16)
            dve.wait_ge(sem.attn_in, 16)
            dve.wait_ge(sem.consts_in, 16)
            dve.tensor_tensor(w3g[:, :], fw["s3"], gv[:, 1:2], ALU.mult).then_inc(sem.vec, 1)
            dve.wait_ge(sem.vec, 12)
            dve.tensor_scalar(diag[:, 0, :], ident, w3g[:, 0:1], None, ALU.mult).then_inc(sem.vec, 1)
            dve.wait_ge(sem.vec, 13)
            dve.tensor_scalar(diag[:, 1, :], ident, gv[:, 3:4], None, ALU.mult).then_inc(sem.diag_ready, 1)
            dve.wait_ge(sem.diag_ready, 1)
            dve.tensor_scalar(hs[:, :], fw["s1"], 0.5, None, ALU.mult).then_inc(sem.vec, 1)
            dve.wait_ge(sem.vec, 14)
            dve.tensor_tensor(ss[:, :], hs[:, :], fw["s2"], ALU.mult).then_inc(sem.vec, 1)
            dve.wait_ge(sem.vec, 15)
            dve.tensor_scalar(kb_lo[:, :], aw["kb1"], cw["lo_k"], None, ALU.mult).then_inc(sem.vec, 1)
            dve.wait_ge(sem.vec, 16)
            dve.tensor_scalar(qb_lo[:, :], aw["qb1"], cw["lo_q"], None, ALU.mult).then_inc(sem.vec, 1)
            dve.wait_ge(sem.vec, 17)
            dve.tensor_scalar(kb_one[:, :], aw["kb1"], cw["one_rows"], None, ALU.add).then_inc(sem.vec, 1)
            dve.wait_ge(sem.vec, 18)
            dve.tensor_tensor(fcbg[:, :], aw["fcb"], gv[:, 2:3], ALU.mult).then_inc(sem.vec, 1)
            dve.wait_ge(sem.vec, 19)
            for b in range(TB):
                dve.wait_ge(sem.idft_ready, b + 1)
                xt = x[:, 4 * b:4 * b + 4, :]
                dve.tensor_tensor(xt, tiles4(bank((5 + b) % 8)), xt, ALU.add).then_inc(sem.x1_ready, 1)
                dve.wait_ge(sem.x1_ready, b + 1)
                ln_stats(1, b)
            ln(1)
            dve.wait_ge(sem.bcast_copied, 2)

            def second_parts(k):
                first, second = hT0 if k == 1 else hT1
                for b in range(TB):
                    block = slice(512 * b, 512 * b + 512)
                    dve.wait_ge(sem.hT_first, TB * (k // 2) + b + 1)
                    dve.tensor_tensor(second[:, block], hT[:, block], first[:, block].bitcast(F32),
                                      ALU.subtract).then_inc(sem.hT_second, 1)

            dve.wait_ge(sem.w_first, 2)
            for i in range(2):
                dve.tensor_tensor(w1_[1][:, i, :], fw[("w1", "w2")[i]], w1_[0][:, i, :].bitcast(F32),
                                  ALU.subtract).then_inc(sem.w_second, 1)
            second_parts(1)
            dve.wait_ge(sem.w_first, 3)
            dve.tensor_tensor(h1_[1][:, :], fw["h1"], h1_[0][:, :].bitcast(F32), ALU.subtract) \
               .then_inc(sem.w_second, 1)

            def ffn_gates(tb):
                def second_part(fb):
                    dve.wait_ge(sem.ah_ready, 4 * tb + fb + 1)
                    dve.tensor_tensor(act_a[1][:, fb, :], af[:, fb % 2, :], act_a[0][:, fb, :].bitcast(F32),
                                      ALU.subtract).then_inc(sem.a_ready, 1)

                for fb in range(FB):
                    n = 4 * tb + fb + 1
                    dve.wait_ge(sem.t_ready, n)
                    dve.scalar_tensor_tensor(out=ug[:, fb % 2, :], in0=tanh_t[:, fb % 2, :], scalar=1.0,
                                             in1=bank(fb % 2), op0=ALU.add, op1=ALU.mult).then_inc(sem.ug_ready, 1)
                    dve.wait_ge(sem.ug_ready, n)
                    if due(n - 2):
                        dve.wait_ge(sem.a_ready, n - 2)
                    dve.scalar_tensor_tensor(out=af[:, fb % 2, :], in0=ug[:, fb % 2, :], scalar=ss[:, fb:fb + 1],
                                             in1=bank(2 + fb % 2), op0=ALU.mult, op1=ALU.mult) \
                       .then_inc(sem.af_ready, 1)
                    if fb:
                        second_part(fb - 1)
                second_part(FB - 1)

            def ffn_b(tb):
                for ob in range(FB):
                    dve.wait_ge(sem.hb_free, 8 * tb + ob + 1)
                    dve.tensor_tensor(act_b[1][:, ob, :], bf[:, ob % 2, :], act_b[0][:, ob, :].bitcast(F32),
                                      ALU.subtract).then_inc(sem.b_ready, 1)

            def ffn_out(tb):
                dve.wait_ge(sem.w3_ready, tb + 1)
                if due(tb):
                    dve.wait_ge(sem.x2_ready, tb)
                dve.tensor_tensor(w3t[:, :, :], tiles4(bank(6)), wide(gb[:, 0, :], [P, 4, P], 1),
                                  ALU.mult).then_inc(sem.w3_scaled, 1)
                dve.wait_ge(sem.w3_scaled, tb + 1)
                xt = x[:, cols(tb, 4), :]
                dve.tensor_tensor(xt, xt, w3t[:, :, :], ALU.add).then_inc(sem.x2_ready, 1)

            ffn_gates(0)
            ffn_b(0)
            ffn_gates(1)
            with dve.Fori(1, TB - 1) as tb:
                ffn_b(tb)
                ffn_out(tb - 1)
                ffn_gates(tb + 1)
            ffn_b(TB - 1)
            ffn_out(TB - 2)
            dve.wait_ge(sem.x2_ready, TB - 1)
            for b in range(TB - 1):
                ln_stats(2, b)
            ffn_out(TB - 1)
            dve.wait_ge(sem.x2_ready, TB)
            ln_stats(2, TB - 1)
            ln(2)
            def stack(n):
                kq, hg, tb = stacks[n]
                dve.wait_ge(sem.kq_hi, n + 1)
                dve.scalar_tensor_tensor(out=(Ks, Qs)[kq][:, hg, tb * 512:tb * 512 + 512], in0=bank(4 + n % 4),
                                         scalar=(kb_one, aw["qb1"])[kq][:, hg:hg + 1], in1=hi[:, n % 2, :].bitcast(F32),
                                         op0=ALU.add, op1=ALU.subtract).then_inc(sem.kq_done, 1)

            def value_tiles(u):
                dve.wait_ge(sem.v_ready, u + 1)
                dve.tensor_tensor(V[:, 2 * u:2 * u + 2, :], bank(4 + u % 4).rearrange("p (t n) -> p t n", t=2),
                                  wide(aw["vb1"], [P, 2, H1 * VW], 1), ALU.add).then_inc(sem.v_copied, 1)

            def maxima(qb, k, pairs=(0, 1)):
                for pair in pairs:
                    dve.wait_ge(sem.nat_ready, 2 * (64 * qb + k) + pair + 1)
                    dve.tensor_reduce(mx[:, k // 16 % 2, k % 16, pair:pair + 1],
                                      ps[:, 2 * pair:2 * pair + 2, :].rearrange("p b n -> p (b n)"), AX, ALU.max) \
                       .then_inc(sem.nat_max, 1)

            def minus_max(qb, grp):
                at = 4 * (4 * qb + grp)
                dve.wait_ge(sem.nat_max, 32 * (4 * qb + grp + 1))
                dve.tensor_reduce(mn[:, :], mx[:, grp % 2, :, :], AX, ALU.max).then_inc(sem.m_step, 1)
                dve.wait_ge(sem.m_step, at + 1)
                dve.tensor_scalar(mhi[:, :], mn[:, :], -1.0, None, ALU.mult).then_inc(sem.m_step, 1)
                dve.wait_ge(sem.m_step, at + 2)
                mn4 = mn[:, :].rearrange("p (q g) -> p q g", g=G4)
                dve.tensor_scalar(m2[:, :, 0:4], mn4, -1.0, None, ALU.mult).then_inc(sem.m_step, 1)
                dve.wait_ge(sem.m_step, at + 3)
                dve.scalar_tensor_tensor(out=m2[:, :, 4:8], in0=mn4, scalar=-1.0,
                                                   in1=mhi[:, :].bitcast(F32).rearrange("p (q g) -> p q g", g=G4),
                                                   op0=ALU.mult, op1=ALU.subtract).then_inc(sem.m_step, 1)
                dve.wait_ge(sem.m_step, at + 4)

            def copy_max_rows(qb, grp):
                dve.wait_ge(sem.mT_ready, 4 * qb + grp + 1)
                if due(128 * (4 * qb + grp)):
                    dve.wait_ge(sem.mrow_in, 128 * (4 * qb + grp))
                dve.tensor_copy(mT[:, :], ps[0:8, 7, :]).then_inc(sem.mT_copied, 1)

            def normalise(qb, grp):
                done = 4 * qb + grp
                dve.wait_ge(sem.uT_ready, done)
                turned = bank(7).rearrange("p (q g w) -> p q g w", q=4, g=G4)
                dve.reciprocal(rden[:, :, :], turned[:, :, :, D1]).then_inc(sem.u_rcp, 1)
                dve.wait_ge(sem.u_rcp, done)
                hg = (grp - 1) % 4
                to = z[:, cols(qb, 4), hg * 32:hg * 32 + 32].rearrange("p q (g w) -> p q g w", w=D1)
                dve.tensor_tensor(to, turned[:, :, :, 0:D1], wide(rden[:, :, :], [P, 4, G4, D1], 3), ALU.mult) \
                   .then_inc(sem.o_norm, 1)

            def step(qb, s):
                kt, grp = s % 16, s // 16
                last_block = isinstance(qb, int) and qb == TB - 1
                ahead = not (last_block and s + LEAD >= 64)
                if ahead:
                    maxima(qb, s + LEAD, (0,))
                if kt == turn_kt and not (isinstance(qb, int) and qb == 0 and s < 16):
                    normalise(qb, grp)
                if kt == rows_kt and not (last_block and grp == 3):
                    copy_max_rows(qb, grp + 1)
                if ahead:
                    maxima(qb, s + LEAD, (1,))
                if kt == rows_kt - 2 and not (last_block and grp == 3):
                    minus_max(qb, grp + 1)

            for n in range(early):
                stack(n)
            for k in range(16):
                for half in range(2):
                    maxima(0, k, (half,))
                    some_stacks, some_values = between(2 * k + half)
                    for n in some_stacks:
                        stack(n)
                    for u in some_values:
                        value_tiles(u)
            minus_max(0, 0)
            maxima(0, 16)
            copy_max_rows(0, 0)
            dve.wait_ge(sem.v_copied, NT // 2)
            dve.memset(bank(6), 0.0).then_inc(sem.o_norm, 1)
            for k in range(17, LEAD):
                maxima(0, k)
            for s in range(4):
                step(0, s)
            with dve.Fori(0, TB - 1) as qb:
                for s in range(4, 68):
                    step(qb, s)
            for s in range(4, 64):
                step(TB - 1, s)
            normalise(TB - 1, 4)

            dve.wait_ge(sem.e_first, 1)
            dve.tensor_tensor(rw1_[1][:, :], mw["rw1"], rw1_[0][:, :].bitcast(F32), ALU.subtract) \
               .then_inc(sem.e_second, 1)
            for b in range(TB):
                dve.wait_ge(sem.yn_ready, b + 1)
                xt = x[:, 4 * b:4 * b + 4, :]
                dve.tensor_tensor(xt, tiles4(bank(4 + b % 2)), xt, ALU.add).then_inc(sem.aux_ready, 1)
                dve.wait_ge(sem.aux_ready, b + 1)
                ln_stats(3, b)
                for e in range(2 * b, 2 * b + 2):
                    at = slice(e * FF, e * FF + FF)
                    dve.wait_ge(sem.e_first, e + 2)
                    dve.tensor_tensor(ew1_[1][:, at], mw["ew1"][:, at], ew1_[0][:, at].bitcast(F32), ALU.subtract) \
                       .then_inc(sem.e_second, 1)
            ln(3)
            second_parts(3)

            def moe(tb):
                ranks = [P, 4, EXP, EXP]
                dve.wait_ge(sem.scT_ready, tb + 1)
                dve.tensor_tensor(sc[:, :, :], ps[:, 6, 0:32].rearrange("p (q e) -> p q e", e=EXP),
                                    wide(mw["rb2"], [P, 4, EXP], 1), ALU.add).then_inc(sem.gt_step, 1)
                dve.wait_ge(sem.gt_step, 13 * tb + 1)
                other, own = wide(sc[:, :, :], ranks, 2), wide(sc[:, :, :], ranks, 3)
                dve.tensor_tensor(cmp[:, :, :, :], other, own, ALU.is_gt).then_inc(sem.gt_step, 1)
                dve.wait_ge(sem.gt_step, 13 * tb + 2)
                dve.tensor_tensor(tie[:, :, :, :], other, own, ALU.is_equal).then_inc(sem.gt_step, 1)
                dve.wait_ge(sem.gt_step, 13 * tb + 3)
                before = wide(cw["before"].rearrange("p (e j) -> p e j", e=EXP), ranks, 1)
                dve.tensor_tensor(tie[:, :, :, :], tie[:, :, :, :], before, ALU.mult).then_inc(sem.gt_step, 1)
                dve.wait_ge(sem.gt_step, 13 * tb + 4)
                dve.tensor_tensor(cmp[:, :, :, :], cmp[:, :, :, :], tie[:, :, :, :], ALU.add).then_inc(sem.gt_step, 1)
                dve.wait_ge(sem.gt_step, 13 * tb + 5)
                dve.tensor_reduce(rank[:, :, :], cmp[:, :, :, :], AX, ALU.add).then_inc(sem.gt_step, 1)
                dve.wait_ge(sem.gt_step, 13 * tb + 6)
                dve.tensor_reduce(top[:, :], sc[:, :, :], AX, ALU.max).then_inc(sem.gt_step, 1)
                dve.wait_ge(sem.gt_step, 13 * tb + 7)
                dve.tensor_tensor(sc[:, :, :], sc[:, :, :], wide(top[:, :], [P, 4, EXP], 2), ALU.subtract).then_inc(sem.gt_step, 1)
                dve.wait_ge(sem.gt_step, 13 * tb + 8)
                dve.tensor_scalar(rank[:, :, :], rank[:, :, :], 2.0, None, ALU.is_lt).then_inc(sem.gt_step, 1)
                dve.wait_ge(sem.gt_step, 13 * tb + 9)
                dve.wait_ge(sem.gate_ready, tb + 1)
                dve.tensor_tensor(gate[:, :, :], gate[:, :, :], rank[:, :, :], ALU.mult).then_inc(sem.gt_step, 1)
                dve.wait_ge(sem.gt_step, 13 * tb + 10)
                dve.tensor_reduce(gs[:, :], gate[:, :, :], AX, ALU.add).then_inc(sem.gt_step, 1)
                dve.wait_ge(sem.gt_step, 13 * tb + 11)
                dve.reciprocal(gs[:, :], gs[:, :]).then_inc(sem.gt_step, 1)
                dve.wait_ge(sem.gt_step, 13 * tb + 12)
                dve.tensor_tensor(gate[:, :, :], gate[:, :, :], wide(gs[:, :], [P, 4, EXP], 2), ALU.mult).then_inc(sem.gt_step, 1)
                dve.wait_ge(sem.gt_step, 13 * tb + 13)
                dve.wait_ge(sem.b2_ready, tb + 1)
                dve.tensor_copy(acc[:, :, :], tiles4(bank(7))).then_inc(sem.acc_ready, 1)
                for e in range(EXP):
                    dve.wait_ge(sem.ey_ready, 8 * tb + e + 1)
                    if e == 0:
                        dve.wait_ge(sem.acc_ready, tb + 1)
                    else:
                        dve.wait_ge(sem.acc_step, 4 * (8 * tb + e))
                    for qt in range(4):
                        dve.scalar_tensor_tensor(out=acc[:, qt, :], in0=ps[:, 2 + e % 2, qt * P:qt * P + P],
                                                 scalar=gate[:, qt, e:e + 1], in1=acc[:, qt, :],
                                                 op0=ALU.mult, op1=ALU.add).then_inc(sem.acc_step, 1)
                dve.wait_ge(sem.acc_step, 4 * (8 * tb + 8))
                dve.tensor_tensor(acc[:, :, :], acc[:, :, :], wide(gb[:, 1, :], [P, 4, P], 1), ALU.mult).then_inc(sem.out_ready, 1)
                dve.wait_ge(sem.out_ready, tb + 1)
                xt = x[:, cols(tb, 4), :]
                dve.tensor_tensor(xt, xt, acc[:, :, :], ALU.add).then_inc(sem.x3_ready, 1)
                dve.wait_ge(sem.x3_ready, tb + 1)

            moe(0)
            with dve.Fori(1, TB) as tb:
                moe(tb)


def _pack(pack, parts):
    cols = []
    for name, n in pack:
        a = np.asarray(parts[name], np.float32)
        full = np.zeros((P, n), np.float32)
        full[:a.shape[0], :] = a
        cols.append(full)
    return np.ascontiguousarray(np.concatenate(cols, 1))


def _constants():
    n, f = np.arange(C)[:, None], np.arange(M)[None, :]
    angle = 2 * np.pi * ((n * f) % C) / C
    forward = np.concatenate([np.cos(angle), -np.sin(angle)], 1)
    weight = np.where((f == 0) | (f == M - 1), 1.0, 2.0) / C
    back = np.concatenate([np.cos(angle) * weight, (-np.sin(angle) * weight)[:, 1:M - 1]], 1).T
    dft, idft = np.zeros((P, 4 * M)), np.zeros((P, P))
    for c in range(2):
        dft[c * C:c * C + C, c * 2 * M:(c + 1) * 2 * M] = forward
        idft[c * C:c * C + C, c * C:c * C + C] = back
    blocks, token = np.arange(NCH)[:, None], np.arange(P)[None, :] // KL
    row = np.arange(P) % 32 // D1
    return {
        "dft": dft, "idft": idft, "ident": np.eye(P), "ones": np.ones((P, P)),
        "mask_row": (token == blocks), "mask_col": np.tile(np.where(token > blocks, -1e30, 0.0), (1, 4)),
        "before": np.tile(np.tril(np.ones((EXP, EXP)), -1).reshape(1, -1), (P, 1)),
        "lo_q": (row == 1)[:, None], "lo_k": (row == 2)[:, None],
        "one_rows": ((np.arange(P) % 32 == 24) | (np.arange(P) % 32 == 25))[:, None],
    }


def _columns(a):
    return a.reshape(-1, P).T


def _blocks(a):
    return a.reshape(-1, P, a.shape[-1]).transpose(1, 0, 2).reshape(P, -1)


def _stack(w):
    out = np.zeros((HG, G4, 32) + w.shape[2:], np.float32)
    for part in range(3):
        out[:, :, part * D1:(part + 1) * D1] = w.reshape((HG, G4) + w.shape[1:])
    return out.reshape((HG, P) + w.shape[2:])


def kernel(**inputs):
    import concourse.bacc as _bacc
    from concourse import mybir as _mybir
    from concourse.bass_utils import run_bass_kernel_spmd as _run

    i = {k: np.asarray(v) for k, v in inputs.items()}
    consts = _constants()
    q = i["L0_attn_q_w"].reshape(2, 2, G4, HD, P).transpose(0, 2, 1, 3, 4).reshape(HEADS * HD, P)
    o = i["L0_attn_o_w"].reshape(P, 2, 2, G4, HD).transpose(1, 3, 2, 4, 0).reshape(HEADS * HD, P)
    mods = dict(consts, c=np.concatenate([i["L0_c"], i["L1_c"]], 0).T, wmod0=i["L0_wmod"], wmod1=i["L1_wmod"])
    spectral = {
        "qw": q.T, "kw": i["L0_attn_k_w"].T, "vw": i["L0_attn_v_w"].T, "ow": _blocks(o),
        "dw_r": i["L0_attn_dw_r"][:, 0], "dw_i": i["L0_attn_dw_i"][:, 0], "pw_r": i["L0_attn_pw_r"].T,
        "pw_i": i["L0_attn_pw_i"].T, "gate_w": i["L0_attn_gate_w"].T,
        "alpha": np.broadcast_to(i["L0_attn_alpha_raw"][None], (P, 1)),
    }
    ffn = {
        "w1": i["L0_ffn_w1_w"].T, "w2": i["L0_ffn_w2_w"].T, "h1": _blocks(i["L0_ffn_h1_w"].T),
        "h2": _blocks(i["L0_ffn_h2_w"].T), "w3": _blocks(i["L0_ffn_w3_w"].T), "s1": _columns(i["L0_ffn_w1_s"]),
        "s2": _columns(i["L0_ffn_w2_s"]), "hs1": _columns(i["L0_ffn_h1_s"]), "hs2": _columns(i["L0_ffn_h2_s"]),
        "s3": _columns(i["L0_ffn_w3_s"]),
    }
    qkv = i["L1_attn_qkv_w"].reshape(H1, 3, D1, P)
    qkv_b = i["L1_attn_qkv_b"].reshape(H1, 3, D1)
    vw = np.zeros((P, H1, VW), np.float32)
    vb = np.zeros((P, H1, VW), np.float32)
    vw[:, :, 0:D1] = qkv[:, 2].transpose(2, 0, 1)
    vb[:, :, 0:D1] = qkv_b[:, 2]
    vb[:, :, D1] = 1.0
    attn = {
        "kw1": _stack(qkv[:, 1]).transpose(2, 0, 1).reshape(P, -1),
        "qw1": _stack(qkv[:, 0]).transpose(2, 0, 1).reshape(P, -1),
        "vw1": vw.reshape(P, -1), "vb1": vb.reshape(P, -1), "kb1": _stack(qkv_b[:, 1]).T,
        "qb1": _stack(qkv_b[:, 0]).T, "fc": i["L1_attn_fc_w"].T, "fcb": _columns(i["L1_attn_fc_b"]),
    }
    moe = {
        "rw1": i["L1_ffn_rw1"], "rb1": _columns(i["L1_ffn_rb1"]), "rw2": _blocks(i["L1_ffn_rw2"]),
        "rb2": np.broadcast_to(i["L1_ffn_rb2"][None], (P, EXP)),
        "ew1": i["L1_ffn_W1"].transpose(1, 0, 2).reshape(P, -1), "eb1": _columns(i["L1_ffn_b1"].reshape(-1)),
        "ew2": _blocks(i["L1_ffn_W2"].reshape(EXP * FF, P)), "eb2": i["L1_ffn_b2"],
    }
    arrays = {
        "x_in": np.ascontiguousarray(i["L0_attn_hidden_states"].reshape(TOK, P)),
        "consts_in": _pack(CONSTS, consts), "mods_in": _pack(MODS, mods), "spectral_in": _pack(SPECTRAL, spectral),
        "ffn_in": _pack(FFN, ffn), "attn_in": _pack(ATTN, attn), "moe_in": _pack(MOE, moe),
    }
    nc = _bacc.Bacc("TRN2", target_bir_lowering=False, num_devices=1)
    args = [nc.dram_tensor(n, a.shape, _mybir.dt.from_np(a.dtype), kind="ExternalInput").ap()
            for n, a in arrays.items()]
    out = nc.dram_tensor("out", (TOK, P), _mybir.dt.float32, kind="ExternalOutput").ap()
    adaln_pair(nc, *args, out)
    r = _run(nc, [arrays], core_ids=[0])
    return np.asarray(r.results[0]["out"]).reshape(1, TOK, P)
```
